# Optimizing a Trainium2 kernel written in Bass

```python
import numpy as np
import jax
import jax.numpy as jnp

def _softmax(x, axis=-1):
    return jax.nn.softmax(x, axis=axis)
def _gelu(x):
    return jax.nn.gelu(x, approximate=True)
def _silu(x):
    return jax.nn.silu(x)
def _sigmoid(x):
    return jax.nn.sigmoid(x)
def _layernorm(x, axis=-1, eps=1e-5):
    m = jnp.mean(x, axis=axis, keepdims=True)
    v = jnp.var(x, axis=axis, keepdims=True)
    return (x - m) / jnp.sqrt(v + eps)
def _scatter_add(tgt, idx, src, axis=0):
    return tgt.at[idx].add(src)
def _segment_sum(src, seg, n):
    return jax.ops.segment_sum(src, seg, n)

kernel_name = 'mk_adj_resnorm_d4_adj_512_c9a5fb'

def setup_inputs(seed: int = 0):
    np.random.seed(seed)
    _w = jnp.asarray
    def _rec_inputs():
        import jax
        import jax.numpy as jnp
        _gk = jax.random.key(seed)
        x = -0.0005207 + 1.001 * jax.random.normal(jax.random.fold_in(_gk, 1), (2708, 512), jnp.float32)
        _a = jax.random.bernoulli(jax.random.fold_in(_gk, 2), 0.00295421, (2708, 2708))
        _a = jnp.logical_or(_a, jnp.swapaxes(_a, -1, -2))
        _a = jnp.logical_or(_a, jnp.eye(2708, dtype=bool))
        _af = _a.astype(jnp.float32)
        adj = _af
        return x, adj
    x, adj = _rec_inputs()
    def _L0_gnn_setup():
        import jax, jax.numpy as jnp
        import numpy as np
        N = 4096
        INPUT_DIM = 512
        KEY_DIM = 64
        OUT_DIM = 512
        N_HEADS = 8

        def _xavier_normal(key, shape, gain):
            fan_in, fan_out = (shape[-2], shape[-1])
            std = gain * (2.0 / (fan_in + fan_out)) ** 0.5
            return jax.random.normal(key, shape, dtype=jnp.float32) * std
        key = jax.random.key(seed)
        kx, ka, kk, kq, kv, ko = jax.random.split(key, 6)
        gain = 2.0 ** 0.5
        node_matrix = jax.random.normal(kx, (N, INPUT_DIM), dtype=jnp.float32)
        adjacency_matrix = jax.random.randint(ka, (N, N), 0, 2).astype(jnp.float32)
        Wks = _xavier_normal(kk, (N_HEADS, INPUT_DIM, KEY_DIM), gain)
        Wqs = _xavier_normal(kq, (N_HEADS, INPUT_DIM, KEY_DIM), gain)
        Wvs = _xavier_normal(kv, (N_HEADS, INPUT_DIM, KEY_DIM), gain)
        Wo = _xavier_normal(ko, (N_HEADS, KEY_DIM, OUT_DIM), gain)
        return {'node_matrix': node_matrix, 'adjacency_matrix': adjacency_matrix, 'Wks': Wks, 'Wqs': Wqs, 'Wvs': Wvs, 'Wo': Wo}
    _L0_gnn_all = _L0_gnn_setup()
    _L0_gnn_in = {k: v for k, v in _L0_gnn_all.items() if k in ('Wks', 'Wqs', 'Wvs', 'Wo', )}
    del _L0_gnn_all

    def _L1_gnn_setup():
        import jax, jax.numpy as jnp
        import numpy as np
        N_NODES = 8192
        DIM = 512
        key = jax.random.key(seed)
        k1, k2, k3, k4 = jax.random.split(key, 4)
        x = jax.random.normal(k1, (N_NODES, DIM), dtype=jnp.float32)
        adj = jax.random.uniform(k2, (N_NODES, N_NODES), dtype=jnp.float32)
        bound = 1.0 / np.sqrt(DIM)
        W = jax.random.uniform(k3, (DIM, DIM), minval=-bound, maxval=bound, dtype=jnp.float32)
        b = jax.random.uniform(k4, (DIM,), minval=-bound, maxval=bound, dtype=jnp.float32)
        return {'x': x, 'adj': adj, 'W': W, 'b': b}
    _L1_gnn_all = _L1_gnn_setup()
    _L1_gnn_in = {k: v for k, v in _L1_gnn_all.items() if k in ('W', 'b', )}
    del _L1_gnn_all

    def _L2_gnn_setup():
        import jax, jax.numpy as jnp
        import numpy as np
        N = 8192
        D_IN = 512
        D_OUT = 512
        NEG_BIG = -9000000000000000.0
        key = jax.random.key(seed)
        kx, ka, kw, kb, kn, ke = jax.random.split(key, 6)
        x = jax.random.normal(kx, (N, D_IN), dtype=jnp.float32)
        adj = (jax.random.uniform(ka, (N, N)) > 0.9).astype(jnp.float32)
        stdv = 1.0 / np.sqrt(D_OUT)
        weight = jax.random.uniform(kw, (D_IN, D_OUT), minval=-stdv, maxval=stdv, dtype=jnp.float32)
        bias = jax.random.uniform(kb, (D_OUT,), minval=-stdv, maxval=stdv, dtype=jnp.float32)
        node_w = jax.random.uniform(kn, (D_IN, 1), minval=-1.0, maxval=1.0, dtype=jnp.float32)
        stdv_e = 1.0 / np.sqrt(D_IN)
        edge_w = jax.random.uniform(ke, (D_IN, D_IN), minval=-stdv_e, maxval=stdv_e, dtype=jnp.float32)
        return {'x': x, 'adj': adj, 'weight': weight, 'bias': bias, 'node_w': node_w, 'edge_w': edge_w}
    _L2_gnn_all = _L2_gnn_setup()
    _L2_gnn_in = {k: v for k, v in _L2_gnn_all.items() if k in ('weight', 'bias', 'node_w', 'edge_w', )}
    del _L2_gnn_all

    def _L3_gnn_setup():
        import jax, jax.numpy as jnp
        import numpy as np
        N = 8192
        D_IN = 512
        D_OUT = 512
        key = jax.random.key(seed)
        k1, k2, k3, k4 = jax.random.split(key, 4)
        x = jax.random.normal(k1, (N, D_IN), dtype=jnp.float32)
        adj = jax.random.uniform(k2, (N, N), dtype=jnp.float32)
        bound = 1.0 / np.sqrt(D_IN)
        W = jax.random.uniform(k3, (D_OUT, D_IN), minval=-bound, maxval=bound, dtype=jnp.float32)
        b = jax.random.uniform(k4, (D_OUT,), minval=-bound, maxval=bound, dtype=jnp.float32)
        return {'x': x, 'adj': adj, 'W': W, 'b': b}
    _L3_gnn_all = _L3_gnn_setup()
    _L3_gnn_in = {k: v for k, v in _L3_gnn_all.items() if k in ('W', 'b', )}
    del _L3_gnn_all

    return {
        "x": x,
        "adj": adj,
        "L0_gnn_Wks": _L0_gnn_in["Wks"],
        "L0_gnn_Wqs": _L0_gnn_in["Wqs"],
        "L0_gnn_Wvs": _L0_gnn_in["Wvs"],
        "L0_gnn_Wo": _L0_gnn_in["Wo"],
        "L1_gnn_W": _L1_gnn_in["W"],
        "L1_gnn_b": _L1_gnn_in["b"],
        "L2_gnn_weight": _L2_gnn_in["weight"],
        "L2_gnn_bias": _L2_gnn_in["bias"],
        "L2_gnn_node_w": _L2_gnn_in["node_w"],
        "L2_gnn_edge_w": _L2_gnn_in["edge_w"],
        "L3_gnn_W": _L3_gnn_in["W"],
        "L3_gnn_b": _L3_gnn_in["b"],
    }

def reference(x, adj, L0_gnn_Wks, L0_gnn_Wqs, L0_gnn_Wvs, L0_gnn_Wo, L1_gnn_W, L1_gnn_b, L2_gnn_weight, L2_gnn_bias, L2_gnn_node_w, L2_gnn_edge_w, L3_gnn_W, L3_gnn_b):
    import jax
    import jax.numpy as jnp
    def _L0_gnn_ref(node_matrix, adjacency_matrix, Wks, Wqs, Wvs, Wo):
        import jax, jax.numpy as jnp
        import numpy as np
        N = 4096
        INPUT_DIM = 512
        KEY_DIM = 64
        OUT_DIM = 512
        N_HEADS = 8

        def _xavier_normal(key, shape, gain):
            fan_in, fan_out = (shape[-2], shape[-1])
            std = gain * (2.0 / (fan_in + fan_out)) ** 0.5
            return jax.random.normal(key, shape, dtype=jnp.float32) * std
        n = adjacency_matrix.shape[0]
        adj = jnp.maximum(adjacency_matrix, jnp.eye(n, dtype=adjacency_matrix.dtype))
        keys = jnp.einsum('nj,hjk->hnk', node_matrix, Wks)
        queries = jnp.einsum('nj,hjk->hnk', node_matrix, Wqs)
        values = jnp.einsum('nj,hjk->hnk', node_matrix, Wvs)
        key_dim = Wks.shape[-1]
        atts = jnp.einsum('hqk,hmk->hqm', queries, keys) / key_dim ** 0.5
        atts = atts - 1e+16 * (1.0 - adj)[None, :, :]
        atts = jax.nn.softmax(atts, axis=-1)
        return jnp.einsum('hqm,hmk,hko->qo', atts, values, Wo)

    def _L1_gnn_ref(x, adj, W, b):
        import jax, jax.numpy as jnp
        import numpy as np
        N_NODES = 8192
        DIM = 512
        agg = jnp.matmul(adj, x)
        out = jnp.matmul(agg, W.T) + b
        return jax.nn.relu(out)

    def _L2_gnn_ref(x, adj, weight, bias, node_w, edge_w):
        import jax, jax.numpy as jnp
        import numpy as np
        N = 8192
        D_IN = 512
        D_OUT = 512
        NEG_BIG = -9000000000000000.0
        node_att = jax.nn.softmax(x @ node_w, axis=0)
        h = x @ edge_w
        e = h @ h.T
        e = jnp.where(adj > 0, e, NEG_BIG)
        edge_att = jax.nn.softmax(e, axis=1)
        combined_att = node_att * edge_att
        support = x @ weight
        output = adj * combined_att @ support
        return output + bias

    def _L3_gnn_ref(x, adj, W, b):
        import jax, jax.numpy as jnp
        import numpy as np
        N = 8192
        D_IN = 512
        D_OUT = 512
        a = adj + jnp.eye(adj.shape[0], dtype=adj.dtype)
        d = jnp.sum(a, axis=1) ** (-0.5)
        a_norm = d[:, None] * a * d[None, :]
        support = a_norm @ x
        out = support @ W.T + b
        out = jax.nn.relu(out)
        return out

    x = _layernorm(x + _L0_gnn_ref(x, adj, L0_gnn_Wks, L0_gnn_Wqs, L0_gnn_Wvs, L0_gnn_Wo), axis=-1)
    x = _layernorm(x + _L1_gnn_ref(x, adj, L1_gnn_W, L1_gnn_b), axis=-1)
    x = _layernorm(x + _L2_gnn_ref(x, adj, L2_gnn_weight, L2_gnn_bias, L2_gnn_node_w, L2_gnn_edge_w), axis=-1)
    x = _layernorm(x + _L3_gnn_ref(x, adj, L3_gnn_W, L3_gnn_b), axis=-1)
    return x


_drawn_inputs = setup_inputs


def setup_inputs(seed=0):
    import zlib

    import numpy as np

    out = dict(_drawn_inputs(seed))
    spreads = {}
    factors = {'L1_gnn_b': 5.702, 'L2_gnn_weight': 8.0, 'L2_gnn_node_w': 7.538, 'L3_gnn_b': 3.54}
    for name, (base, spread) in spreads.items():
        noise = np.random.default_rng([zlib.crc32(name.encode()), seed]).standard_normal(out[name].shape)
        drawn = base * np.exp(spread * noise) if base else spread * noise
        out[name] = jnp.asarray(drawn.astype(out[name].dtype))
    for name, factor in factors.items():
        out[name] = (out[name] * factor).astype(out[name].dtype)
    return out
```

```python
from contextlib import ExitStack

import numpy as np

import concourse.bass as bass
from concourse import mybir

F32 = mybir.dt.float32
F16 = mybir.dt.float16
ALU = mybir.AluOpType
ACT = mybir.ActivationFunctionType
AX = mybir.AxisListType

P = 128
N = 2708
D = 512
H = 8
KD = 64
T = -(-N // P)
NP = T * P
LAST = N - (T - 1) * P
J = D // P
BANK = 512
CHUNK = 2 * BANK
CHUNKS = [(c, min(CHUNK, N - c)) for c in range(0, N, CHUNK)]
NC = len(CHUNKS)
GB = BANK // P
GROUPS = [list(range(g, min(g + GB, T))) for g in range(0, T, GB)]
NG = len(GROUPS)
assert NG == 2 * NC and T % 2 == 0 and N % P

X_S, W_S, Q_S, V_S, P_S, O_S = 16.0, 256.0, 16.0, 16.0, 1024.0, 16.0
XW = 1.0 / (X_S * W_S)
EPS = 1e-5
BIG0 = 1e16
BIG2 = -9000000000000000.0


def wait_apart(eng, sem, value, met):
    if not isinstance(value, int):
        value = eng.to_reg(value)
    eng.wait_ge(met, 1)
    eng.wait_ge(sem, value)


def rows_of(k):
    return P if k < T - 1 else LAST


class Scope:

    def __init__(self, nc, ctx, tag):
        self.nc, self.ctx, self.tag, self.sems = nc, ctx, tag, []
        ctx.callback(self.release)

    def release(self):
        if self.sems:
            self.nc.clear_and_free_semaphores(self.sems)
            self.nc.all_engine_barrier()

    def sb(self, name, shape, dt=F32):
        return self.ctx.enter_context(self.nc.sbuf_tensor(f"{self.tag}_{name}", shape, dt))

    def ps(self, name, shape):
        return self.ctx.enter_context(self.nc.psum_tensor(f"{self.tag}_{name}", shape, F32))

    def sem(self, name):
        self.sems.append(self.nc.alloc_semaphore(f"{self.tag}_{name}"))
        return self.sems[-1]


def product3(nc, out, lhs, rhs, first=True, last=True):
    terms = [(a, b, j) for j in range(J) for a, b in ((0, 0), (0, 1), (1, 0))]
    for n, (a, b, j) in enumerate(terms):
        mm = nc.tensor.matmul(out, lhs(a, j), rhs(b, j), start=first and n == 0,
                              stop=last and n == len(terms) - 1)
    return mm


def split_weights(nc, s, block, jobs):
    loaded, high, low = s.sem("w_loaded"), s.sem("w_high"), s.sem("w_low")

    @block.sync
    def _(sp):
        for src, _h, _l, stage in jobs:
            sp.dma_start(stage, src).then_inc(loaded, 16)

    @block.scalar
    def _(act):
        act.wait_ge(loaded, 16 * len(jobs))
        for _src, h, _l, stage in jobs:
            nc.scalar.activation(h, stage, ACT.Copy, scale=W_S).then_inc(high, 1)

    @block.vector
    def _(dve):
        for n, (_src, h, l, stage) in enumerate(jobs):
            dve.wait_ge(high, n + 1)
            nc.vector.scalar_tensor_tensor(out=l, in0=stage, scalar=W_S, in1=h, op0=ALU.mult,
                                           op1=ALU.subtract).then_inc(low, 1)


def weights_phase(nc, tag, specs):
    with ExitStack() as ctx:
        s = Scope(nc, ctx, tag)
        jobs = []
        for n, (src, h, l) in enumerate(specs):
            stage = s.sb(f"stage{n}", [P, J, src.shape[1]])
            jobs.append((src.rearrange("(j p) n -> p j n", p=P), h, l, stage[:, :, :]))
        block = ctx.enter_context(nc.Block())
        split_weights(nc, s, block, jobs)


def pairs(eng, begin, end, step):
    turns = (end - begin) // 2
    with eng.Fori(0, turns) as i:
        for t in (begin, begin + 1):
            step(i + t // 2, t % 2)
    if (end - begin) % 2:
        step((end - 1) // 2, (end - 1) % 2)


def after(m, u):
    return (m, 1) if u == 0 else (m + 1, 0)


def project(nc, tag, x_rows, ident, jobs, score=None, row_scale=None):
    with ExitStack() as ctx:
        s = Scope(nc, ctx, tag)
        x_in = s.sb("x_in", [P, 2, D])
        xt = s.sb("xt", [P, 2, 2, J, P], F16)
        junk = s.sb("junk", [P, D])
        ps_t = s.ps("ps_t", [P, 2, BANK])
        ps_job = [s.ps(f"ps_job{n}", [P, 2, BANK]) for n in range(len(jobs))]
        x_loaded = [s.sem(f"x_loaded{u}") for u in range(2)]
        turned = s.sem("turned")
        xt_high = s.sem("xt_high")
        xt_low = s.sem("xt_low")
        made = s.sem("made")
        out_high = s.sem("out_high")
        out_low = s.sem("out_low")
        weighed = s.sem("weighed")
        scored = s.sem("scored")
        nj = len(jobs)
        block = ctx.enter_context(nc.Block())

        @block.sync
        def _(sp):
            def load(m, u):
                if not (isinstance(m, int) and m == 0):
                    sp.wait_ge(turned, 2 * m + u - 1)
                    if score is not None:
                        sp.wait_ge(scored, 2 * m + u - 1)
                sp.dma_start(x_in[:, u, :], x_rows[bass.ds((2 * m + u) * P, P), :]) \
                    .then_inc(x_loaded[u], 16)

            load(0, 0)
            load(0, 1)
            pairs(sp, 2, T, load)

        @block.tensor
        def _(pe):
            def turn(m, u):
                pe.wait_ge(x_loaded[u], 16 * m + 16)
                if not (isinstance(m, int) and m == 0):
                    pe.wait_ge(xt_low, 2 * m + u - 1)
                for j in range(J):
                    mm = nc.tensor.transpose(ps_t[:, u, j * P:(j + 1) * P],
                                             x_in[:, u, j * P:(j + 1) * P], ident[:, :])
                mm.then_inc(turned, 1)

            def multiply(m, u):
                pe.wait_ge(xt_low, 2 * m + u + 1)
                for n, (kind, wh, wl, _) in enumerate(jobs):
                    w = (wh, wl)
                    if not (isinstance(m, int) and m == 0):
                        pe.wait_ge(out_low, nj * (2 * m + u - 2) + n + 1)
                    if kind == "rows":
                        mm = product3(nc, ps_job[n][:, u, :], lambda a, j: xt[:, u, a, j, :],
                                      lambda b, j: w[b][:, j, :])
                    else:
                        for c in range(J):
                            mm = product3(nc, ps_job[n][:, u, c * P:(c + 1) * P],
                                          lambda a, j: w[a][:, j, c * P:(c + 1) * P],
                                          lambda b, j: xt[:, u, b, j, :])
                    mm.then_inc(made, 1)

            def step(m, u):
                turn(*after(m, u))
                multiply(m, u)

            turn(0, 0)
            step(0, 0)
            step(0, 1)
            pairs(pe, 2, T - 1, step)
            multiply(T // 2 - 1, 1)

        @block.scalar
        def _(act):
            def split(m, u):
                act.wait_ge(turned, 2 * m + u + 1)
                if not (isinstance(m, int) and m == 0):
                    act.wait_ge(made, nj * (2 * m + u - 1))
                nc.scalar.activation(xt[:, u, 0, :, :], ps_t[:, u, :].rearrange("p (j r) -> p j r", j=J),
                                     ACT.Copy, scale=X_S).then_inc(xt_high, 1)

            def finish(m, u):
                t = 2 * m + u
                for n, (_, _, _, pieces) in enumerate(jobs):
                    act.wait_ge(made, nj * t + n + 1)
                    for part, high, _low, scale in pieces(t, ps_job[n][:, u, :]):
                        if row_scale is not None:
                            scale = row_scale[:, bass.ds(t, 1)]
                        op = nc.scalar.activation(high, part, ACT.Copy, scale=scale)
                    op.then_inc(out_high, 1)

            def step(m, u):
                split(*after(m, u))
                finish(m, u)

            split(0, 0)
            step(0, 0)
            pairs(act, 1, T - 1, step)
            finish(T // 2 - 1, 1)

        @block.vector
        def _(dve):
            def split(m, u):
                t = 2 * m + u
                dve.wait_ge(xt_high, t + 1)
                nc.vector.scalar_tensor_tensor(
                    out=xt[:, u, 1, :, :], in0=ps_t[:, u, :].rearrange("p (j r) -> p j r", j=J), scalar=X_S,
                    in1=xt[:, u, 0, :, :], op0=ALU.mult, op1=ALU.subtract).then_inc(xt_low, 1)
                if score is not None:
                    node_w, z = score
                    r = LAST if isinstance(m, int) and t == T - 1 else P
                    dve.wait_ge(x_loaded[u], 16 * m + 16)
                    if not (isinstance(m, int) and t == 0):
                        dve.wait_ge(scored, t)
                    nc.vector.tensor_tensor(out=junk[0:r, :], in0=x_in[0:r, u, :], in1=node_w[0:r, :],
                                            op=ALU.mult).then_inc(weighed, 1)
                    dve.wait_ge(weighed, t + 1)
                    nc.vector.tensor_reduce(out=z[0:r, bass.ds(t, 1)], in_=junk[0:r, :], axis=AX.X,
                                            op=ALU.add).then_inc(scored, 1)

            def finish(m, u):
                t = 2 * m + u
                for n, (_, _, _, pieces) in enumerate(jobs):
                    dve.wait_ge(out_high, nj * t + n + 1)
                    for part, high, low, scale in pieces(t, ps_job[n][:, u, :]):
                        if row_scale is not None:
                            scale = row_scale[:, bass.ds(t, 1)]
                        op = nc.vector.scalar_tensor_tensor(out=low, in0=part, scalar=scale, in1=high,
                                                            op0=ALU.mult, op1=ALU.subtract)
                    op.then_inc(out_low, 1)

            def step(m, u):
                split(*after(m, u))
                finish(m, u)

            split(0, 0)
            step(0, 0)
            pairs(dve, 1, T - 3, step)
            for t in range(T - 3, T - 1):
                step(t // 2, t % 2)
            finish(T // 2 - 1, 1)


def before(m, u):
    return (m, 0) if u == 1 else (m - 1, 1)


def is_tile(m, u, t):
    return isinstance(m, int) and 2 * m + u == t


class Norm:

    def __init__(self, s):
        self.r = s.sb("residual", [P, D])
        self.stats, self.mv = s.sb("stats", [P, 6]), s.sb("mv", [P, 2])
        self.veps, self.rstd = s.sb("veps", [P, 1]), s.sb("rstd", [P, 1])
        self.power = s.sb("power", [P, 1])
        self.out = s.sb("x_out", [P, 2, D])
        self.stats_ready = s.sem("stats_ready")
        self.mv_ready = s.sem("mv_ready")
        self.power_ready = s.sem("power_ready")
        self.veps_ready = s.sem("veps_ready")
        self.rstd_ready = s.sem("rstd_ready")
        self.x_ready = s.sem("x_ready")
        self.stored = [s.sem(f"x_stored{u}") for u in range(2)]

    def statistics(self, nc, dve, t):
        nc.vector.bn_stats(out=self.stats[:, :], in_=self.r[:, :]).then_inc(self.stats_ready, 1)
        wait_apart(dve, self.stats_ready, t + 1, self.power_ready)
        nc.vector.bn_aggr(out=self.mv[:, :], in_=self.stats[:, :]).then_inc(self.mv_ready, 1)

    def exponent(self, nc, pool):
        nc.gpsimd.memset(self.power[:, :], -0.5).then_inc(self.power_ready, 1)
        pool.wait_ge(self.power_ready, 1)

    def deviation(self, nc, pool, t):
        wait_apart(pool, self.mv_ready, t + 1, self.power_ready)
        nc.gpsimd.tensor_scalar(out=self.veps[:, :], in0=self.mv[:, 1:2], scalar1=1.0, scalar2=EPS,
                                op0=ALU.mult, op1=ALU.add).then_inc(self.veps_ready, 1)
        pool.wait_ge(self.veps_ready, t + 1)
        nc.gpsimd.tensor_tensor(out=self.rstd[:, :], in0=self.veps[:, :], in1=self.power[:, :],
                                op=ALU.pow).then_inc(self.rstd_ready, 1)

    def finish(self, nc, dve, m, u):
        dve.wait_ge(self.rstd_ready, 2 * m + u + 1)
        if not (isinstance(m, int) and m == 0):
            dve.wait_ge(self.stored[u], 16 * m)
        nc.vector.tensor_scalar(out=self.out[:, u, :], in0=self.r[:, :], scalar1=self.mv[:, 0:1],
                                scalar2=self.rstd[:, :], op0=ALU.subtract, op1=ALU.mult) \
            .then_inc(self.x_ready, 1)

    def store(self, sp, rows, m, u):
        sp.wait_ge(self.x_ready, 2 * m + u + 1)
        sp.dma_start(rows[bass.ds((2 * m + u) * P, P), :], self.out[:, u, :]).then_inc(self.stored[u], 16)

    def all_stored(self, sp):
        for u in range(2):
            sp.wait_ge(self.stored[u], 16 * (T // 2))


def attention(nc, x_rows, out_rows, adj_rows, kk, vv, wq, wo, ident):
    with ExitStack() as ctx:
        s = Scope(nc, ctx, "att")
        adj = s.sb("adj", [P, 2, NP])
        xq = s.sb("xq", [P, D])
        xres = s.sb("xres", [P, 2, D])
        xt = s.sb("xt", [P, 2, J, P], F16)
        q = [s.sb(f"q{a}", [P, 2, H, P], F16) for a in ("high", "low")]
        sp_sb = s.sb("scores", [P, 2, N])
        pt = [s.sb(f"pt_{a}", [P, NG, BANK], F16) for a in ("high", "low")]
        o_half = s.sb("o_half", [P, 2, KD])
        o = s.sb("o", [P, 2, D])
        ot = s.sb("ot", [P, 2, J, P], F16)
        mx, nmax = s.sb("mx", [P, 2, NC]), s.sb("nmax", [P, 2])
        esum, ssum, rinv = s.sb("esum", [P, 2, NC]), s.sb("ssum", [P, 2]), s.sb("rinv", [P, 2])
        norm = Norm(s)
        slots = s.ps("slots", [P, 2, CHUNK])
        ps_t = s.ps("ps_t", [P, 2, BANK])
        ps_pv = s.ps("ps_pv", [P, 2, BANK])

        adj_loaded = [s.sem(f"adj_loaded{u}") for u in range(2)]
        xres_loaded = [s.sem(f"xres_loaded{u}") for u in range(2)]
        xq_loaded = s.sem("xq_loaded")
        pad_clear = s.sem("pad_clear")
        diag_ready = s.sem("diag_ready")
        bias_ready = s.sem("bias_ready")
        slot_full = s.sem("slot_full")
        slot_high = s.sem("slot_high")
        slot_free = s.sem("slot_free")
        nmax_ready = s.sem("nmax_ready")
        exp_done = s.sem("exp_done")
        turned = s.sem("turned")
        pt_high = s.sem("pt_high")
        pt_low = s.sem("pt_low")
        ssum_ready = s.sem("ssum_ready")
        rinv_ready = s.sem("rinv_ready")
        pv_done = s.sem("pv_done")
        half_done = s.sem("half_done")
        o_done = s.sem("o_done")
        block = ctx.enter_context(nc.Block())

        EXTRA = {3: "ot", 4: "wo", 5: "xt", 6: "q"}
        PER_TILE = NC * H + len(EXTRA)
        assert PER_TILE % 2 == 0

        def extras(m, u):
            have = dict(EXTRA)
            if is_tile(m, u, 0):
                del have[3], have[4]
            if is_tile(m, u, T - 1):
                del have[5], have[6]
            return have

        def slots_of(m, u):
            have = extras(m, u)
            base = 2 if is_tile(m, u, 0) else 0
            place = {}
            for h in range(H):
                for use in [(h, c) for c in range(NC)] + ([have[h]] if h in have else []):
                    place[use] = (2 * m + u) * PER_TILE + base + len(place)
            return place

        def parity(m, u, use):
            place = slots_of(m, u) if isinstance(m, int) else slots_of(1, u)
            return place[use] % 2

        TAIL = {"ot": T * PER_TILE - 2, "wo": T * PER_TILE - 1}
        HEAD = {"xt": 0, "q": 1}

        def tile_steps(m, u, step, extra):
            place = slots_of(m, u)
            for h in range(H):
                first = is_tile(m, u, 0)
                step(m, u, h, place, True, not first or h >= 1, not first or h >= 2, not first or h >= 3)
                if h in extras(m, u):
                    use = extras(m, u)[h]
                    extra(use, m, u, place[use], parity(m, u, use))

        def all_steps(eng, step, extra, around=None):
            tile = lambda m, u: tile_steps(m, u, step, extra)
            extra("xt", -1, 1, HEAD["xt"], 0)
            extra("q", -1, 1, HEAD["q"], 1)
            tile(0, 0)
            pairs(eng, 1, T - 1, tile)
            tile(T // 2 - 1, 1)
            for h, flags in enumerate([(False, True, True, True), (False, False, True, True),
                                       (False, False, False, True)]):
                step(T // 2, 0, h, None, *flags)
            extra("ot", T // 2, 0, TAIL["ot"], 0)
            extra("wo", T // 2, 0, TAIL["wo"], 1)

        @block.sync
        def _(sp):
            sp.dma_start(xq[:, :], x_rows[0:P, :]).then_inc(xq_loaded, 16)
            sp.dma_start(adj[:, 0, 0:N], adj_rows[0:P, :]).then_inc(adj_loaded[0], 16)

            def tile(m, u):
                t = 2 * m + u
                if not is_tile(m, u, 0):
                    sp.wait_ge(slot_free, PER_TILE * t)
                if not is_tile(m, u, T - 1):
                    m1, u1 = after(m, u)
                    sp.dma_start(adj[:, u1, 0:N], adj_rows[bass.ds((t + 1) * P, P), :]) \
                        .then_inc(adj_loaded[u1], 16)
                    if is_tile(m, u, 0):
                        sp.wait_ge(slot_full, 1)
                    sp.dma_start(xq[:, :], x_rows[bass.ds((t + 1) * P, P), :]).then_inc(xq_loaded, 16)
                if not (isinstance(m, int) and m == 0):
                    sp.wait_ge(norm.mv_ready, t - 1)
                sp.dma_start(xres[:, u, :], x_rows[bass.ds(t * P, P), :]).then_inc(xres_loaded[u], 16)
                if not is_tile(m, u, 0):
                    norm.store(sp, out_rows, *(before(m, u)))

            tile(0, 0)
            pairs(sp, 1, T - 1, tile)
            tile(T // 2 - 1, 1)
            norm.store(sp, out_rows, T // 2 - 1, 1)
            norm.all_stored(sp)

        @block.gpsimd
        def _(pool):
            nc.gpsimd.memset(adj[:, :, N:NP], 0.0).then_inc(pad_clear, 1)
            norm.exponent(nc, pool)

            def bias(m, u):
                wait_apart(pool, diag_ready, 2 * m + u + 1, pad_clear)
                big = BIG0 * Q_S * Q_S
                nc.gpsimd.tensor_scalar(out=adj[:, u, 0:N], in0=adj[:, u, 0:N], scalar1=big, scalar2=-big,
                                        op0=ALU.mult, op1=ALU.add).then_inc(bias_ready, 1)

            def tile(m, u):
                if not is_tile(m, u, T - 1):
                    bias(*after(m, u))
                if not is_tile(m, u, 0):
                    norm.deviation(nc, pool, 2 * m + u - 1)

            bias(0, 0)
            tile(0, 0)
            pairs(pool, 1, T - 1, tile)
            tile(T // 2 - 1, 1)
            norm.deviation(nc, pool, T - 1)

        @block.tensor
        def _(pe):
            def values(i, h, g):
                pe.wait_ge(pt_low, NG * i + g + 1)
                b = h % 2
                for k in GROUPS[g]:
                    r = rows_of(k)
                    for a in range(2):
                        mm = nc.tensor.matmul(ps_pv[:, b, 0:P], pt[a][0:r, g, (k % GB) * P:(k % GB + 1) * P],
                                              vv[0:r, k, h, :], start=k == 0 and a == 0,
                                              stop=k == T - 1 and a == 1)
                return mm

            def step(m, u, h, place, scores, _exp, probs, tail):
                i = (2 * m + u) * H + h
                for c, (lo, width) in enumerate(CHUNKS):
                    if probs:
                        pe.wait_ge(exp_done, NC * (i - 2) + c + 1)
                        for g in (2 * c, 2 * c + 1):
                            n = NG * (i - 2) + g
                            if not (isinstance(n, int) and n < 2):
                                pe.wait_ge(pt_low, n - 1)
                            for k in GROUPS[g]:
                                r = rows_of(k)
                                mm = nc.tensor.transpose(ps_t[0:r, g % 2, (k % GB) * P:(k % GB + 1) * P],
                                                         sp_sb[:, h % 2, k * P:k * P + r], ident[:, :])
                            mm.then_inc(turned, 1)
                    if scores:
                        n, slot = place[h, c], parity(m, u, (h, c))
                        if c == 0 and h == 0:
                            if is_tile(m, u, 0):
                                pe.wait_ge(slot_free, 2)
                        pe.wait_ge(slot_free, n - 1)
                        for a in range(2):
                            for z in range(0, width, BANK):
                                w = min(BANK, width - z)
                                mm = nc.tensor.matmul(slots[:, slot, z:z + w], q[a][:, u, h, :],
                                                      kk[:, h, lo + z:lo + z + w],
                                                      start=a == 0, stop=a == 1)
                        mm.then_inc(slot_full, 1)
                    if c == 0:
                        if tail:
                            values(i - 3, (h - 3) % H, NG - 2)
                            values(i - 3, (h - 3) % H, NG - 1).then_inc(pv_done, 1)
                    elif probs:
                        if c == 1 and not (isinstance(i, int) and i < 4):
                            pe.wait_ge(o_done, i - 3)
                        values(i - 2, (h - 2) % H, 2 * c - 2)
                        values(i - 2, (h - 2) % H, 2 * c - 1)

            def extra(use, m, u, n, slot):
                t = 2 * m + u
                if not (isinstance(n, int) and n < 2):
                    pe.wait_ge(slot_free, n - 1)
                out = slots[:, slot, :]
                if use == "ot":
                    pe.wait_ge(o_done, H * t)
                    for j in range(J):
                        mm = nc.tensor.transpose(out[:, j * P:(j + 1) * P], o[:, 1 - u, j * P:(j + 1) * P],
                                                 ident[:, :])
                elif use == "wo":
                    pe.wait_ge(slot_free, n if is_tile(m, u, T) else n - NC)
                    mm = product3(nc, out[:, 0:D], lambda a, j: ot[:, a, j, :], lambda b, j: wo[b][:, j, :])
                elif use == "xt":
                    pe.wait_ge(xq_loaded, 16 * (t + 2))
                    for j in range(J):
                        mm = nc.tensor.transpose(out[:, j * P:(j + 1) * P], xq[:, j * P:(j + 1) * P],
                                                 ident[:, :])
                else:
                    if not (isinstance(n, int) and n < 2):
                        pe.wait_ge(slot_free, n - NC)
                    else:
                        pe.wait_ge(slot_free, 1)
                    for h in range(H):
                        mm = product3(nc, out[:, h * P:(h + 1) * P], lambda a, j: wq[a][:, j, h * P:(h + 1) * P],
                                      lambda b, j: xt[:, b, j, :])
                mm.then_inc(slot_full, 1)

            all_steps(pe, step, extra)

        @block.scalar
        def _(act):
            def step(m, u, h, place, _scores, exp, probs, tail):
                i = (2 * m + u) * H + h
                for c, (lo, width) in enumerate(CHUNKS):
                    if probs:
                        for g in (2 * c, 2 * c + 1):
                            act.wait_ge(turned, NG * (i - 2) + g + 1)
                            w = P * len(GROUPS[g])
                            nc.scalar.activation(pt[0][:, g, 0:w], ps_t[:, g % 2, 0:w], ACT.Copy, scale=P_S) \
                                .then_inc(pt_high, 1)
                    if tail and c == 1:
                        b = (h - 3) % 2
                        act.wait_ge(pv_done, i - 2)
                        act.wait_ge(rinv_ready, i - 2)
                        nc.scalar.activation(o_half[:, b, :], ps_pv[:, b, 0:KD], ACT.Copy,
                                             scale=rinv[:, b:b + 1]).then_inc(half_done, 1)
                    if exp:
                        b = (h - 1) % 2
                        if c == 0:
                            act.wait_ge(nmax_ready, i)
                        nc.scalar.activation(sp_sb[:, b, lo:lo + width], sp_sb[:, b, lo:lo + width], ACT.Exp,
                                             bias=nmax[:, b:b + 1], accum_out=esum[:, b, c:c + 1]) \
                            .then_inc(exp_done, 1)

            def extra(use, m, u, n, slot):
                if use == "wo":
                    return
                act.wait_ge(slot_full, n + 1)
                src = slots[:, slot, :]
                if use == "q":
                    nc.scalar.activation(q[0][:, 1 - u, :, :], src.rearrange("p (h r) -> p h r", h=H), ACT.Copy,
                                         scale=Q_S / 8.0 * XW).then_inc(slot_high, 1)
                else:
                    dst, scale = (ot, O_S / (P_S * V_S)) if use == "ot" else (xt, X_S)
                    nc.scalar.activation(dst[:, 0, :, :], src[:, 0:D].rearrange("p (j r) -> p j r", j=J),
                                         ACT.Copy, scale=scale).then_inc(slot_high, 1)

            all_steps(act, step, extra)

        @block.vector
        def _(dve):
            def step(m, u, h, place, scores, _exp, probs, tail):
                i = (2 * m + u) * H + h
                for c, (lo, width) in enumerate(CHUNKS):
                    if probs:
                        for g in (2 * c, 2 * c + 1):
                            dve.wait_ge(pt_high, NG * (i - 2) + g + 1)
                            w = P * len(GROUPS[g])
                            nc.vector.scalar_tensor_tensor(
                                out=pt[1][:, g, 0:w], in0=ps_t[:, g % 2, 0:w], scalar=P_S,
                                in1=pt[0][:, g, 0:w], op0=ALU.mult, op1=ALU.subtract).then_inc(pt_low, 1)
                        b = h % 2
                        if c == 0:
                            dve.wait_ge(exp_done, NC * (i - 1))
                            nc.vector.tensor_reduce(out=ssum[:, b:b + 1], in_=esum[:, b, :], axis=AX.X,
                                                    op=ALU.add).then_inc(ssum_ready, 1)
                        if c == 2:
                            dve.wait_ge(ssum_ready, i - 1)
                            nc.vector.reciprocal(rinv[:, b:b + 1], ssum[:, b:b + 1]).then_inc(rinv_ready, 1)
                    if scores:
                        n, slot = place[h, c], parity(m, u, (h, c))
                        if h == 0 and c == 0:
                            dve.wait_ge(bias_ready, 2 * m + u + 1)
                        wait_apart(dve, slot_full, n + 1, pad_clear)
                        nc.vector.tensor_tensor_reduce(
                            out=sp_sb[:, h % 2, lo:lo + width], in0=slots[:, slot, 0:width],
                            in1=adj[:, u, lo:lo + width], scale=1.0 / (Q_S * Q_S), scalar=-3.0e38,
                            op0=ALU.add, op1=ALU.max, accum_out=mx[:, h % 2, c:c + 1]).then_inc(slot_free, 1)
                    if tail and c == 1:
                        b, head = (h - 3) % 2, (h - 3) % H
                        ou = u if h >= 3 else 1 - u
                        dve.wait_ge(half_done, i - 2)
                        nc.vector.scalar_tensor_tensor(
                            out=o[:, ou, head * KD:(head + 1) * KD], in0=ps_pv[:, b, KD:2 * KD],
                            scalar=rinv[:, b:b + 1], in1=o_half[:, b, :], op0=ALU.mult, op1=ALU.add) \
                            .then_inc(o_done, 1)
                if scores:
                    dve.wait_ge(slot_free, place[h, NC - 1] + 1)
                    nc.vector.tensor_reduce(out=nmax[:, h % 2:h % 2 + 1], in_=mx[:, h % 2, :], axis=AX.X,
                                            op=ALU.max, negate=True).then_inc(nmax_ready, 1)
                    if h == 1 and not is_tile(m, u, T - 1):
                        diagonal(*after(m, u))
                    if h == 5 and not is_tile(m, u, 0):
                        norm.finish(nc, dve, *before(m, u))

            def diagonal(m, u):
                t = 2 * m + u
                dve.wait_ge(adj_loaded[u], 16 * m + 16)
                part = adj[:, u, bass.ds(t * P, P)]
                nc.vector.tensor_tensor(out=part, in0=part, in1=ident[:, :], op=ALU.max) \
                    .then_inc(diag_ready, 1)

            def highs(use, m, u):
                t = 2 * m + u
                if is_tile(m, u, -1):
                    return {"xt": 1, "q": 2}[use]
                if is_tile(m, u, T):
                    return 3 * T
                return 3 * t + {"ot": 2, "xt": 3, "q": 4}[use]

            def extra(use, m, u, n, slot):
                t = 2 * m + u
                src = slots[:, slot, :]
                if use == "wo":
                    um = 1 - u
                    m1, _ = before(m, u)
                    dve.wait_ge(slot_full, n + 1)
                    dve.wait_ge(xres_loaded[um], 16 * m1 + 16)
                    nc.vector.scalar_tensor_tensor(out=norm.r[:, :], in0=src[:, 0:D], scalar=1.0 / (O_S * W_S),
                                                   in1=xres[:, um, :], op0=ALU.mult, op1=ALU.add) \
                        .then_inc(slot_free, 1)
                    dve.wait_ge(slot_free, n + 1)
                    norm.statistics(nc, dve, t - 1)
                    return
                dve.wait_ge(slot_high, highs(use, m, u))
                if use == "q":
                    nc.vector.scalar_tensor_tensor(
                        out=q[1][:, 1 - u, :, :], in0=src.rearrange("p (h r) -> p h r", h=H),
                        scalar=Q_S / 8.0 * XW, in1=q[0][:, 1 - u, :, :], op0=ALU.mult,
                        op1=ALU.subtract).then_inc(slot_free, 1)
                else:
                    dst, scale = (ot, O_S / (P_S * V_S)) if use == "ot" else (xt, X_S)
                    nc.vector.scalar_tensor_tensor(
                        out=dst[:, 1, :, :], in0=src[:, 0:D].rearrange("p (j r) -> p j r", j=J), scalar=scale,
                        in1=dst[:, 0, :, :], op0=ALU.mult, op1=ALU.subtract).then_inc(slot_free, 1)

            dve.wait_ge(pad_clear, 1)
            diagonal(0, 0)
            all_steps(dve, step, extra)
            norm.finish(nc, dve, T // 2 - 1, 1)


def edge_attention(nc, x_rows, out_rows, adj_rows, ht, sup, natt, bias_row, degree, ident):
    with ExitStack() as ctx:
        s = Scope(nc, ctx, "edge")
        adj = s.sb("adj", [P, 2, N])
        bias = s.sb("bias", [P, N])
        xres = s.sb("xres", [P, 2, D])
        sc = s.sb("scores", [P, 2, N])
        pt = [s.sb(f"pt_{a}", [P, 2, BANK], F16) for a in ("high", "low")]
        xb = s.sb("xb", [P, 2, D])
        mx, nmax = s.sb("mx", [P, NC]), s.sb("nmax", [P, 1])
        esum, ssum, rinv = s.sb("esum", [P, 2, NC]), s.sb("ssum", [P, 1]), s.sb("rinv", [P, 1])
        rscale = s.sb("rscale", [P, 2])
        norm = Norm(s)
        slots = s.ps("slots", [P, 2, CHUNK])
        ps_t = s.ps("ps_t", [P, 2, BANK])
        ps_o = s.ps("ps_o", [P, 2, BANK])

        adj_loaded = [s.sem(f"adj_loaded{u}") for u in range(2)]
        xres_loaded = [s.sem(f"xres_loaded{u}") for u in range(2)]
        bias_ready = s.sem("bias_ready")
        slot_full = s.sem("slot_full")
        slot_free = s.sem("slot_free")
        nmax_ready = s.sem("nmax_ready")
        exp_done = s.sem("exp_done")
        weighed = s.sem("weighed")
        degree_ready = s.sem("degree_ready")
        ssum_ready = s.sem("ssum_ready")
        rinv_ready = s.sem("rinv_ready")
        rscale_ready = s.sem("rscale_ready")
        turned = s.sem("turned")
        pt_high = s.sem("pt_high")
        pt_low = s.sem("pt_low")
        used = s.sem("used")
        xb_ready = s.sem("xb_ready")
        r_ready = s.sem("r_ready")
        block = ctx.enter_context(nc.Block())

        def tiles(eng, front, back):
            def both(m, u):
                front(m, u)
                back(*before(m, u))

            front(0, 0)
            both(0, 1)
            pairs(eng, 2, T - 1, both)
            both(T // 2 - 1, 1)
            back(T // 2 - 1, 1)

        @block.sync
        def _(sp):
            def front(m, u):
                if not (isinstance(m, int) and m == 0):
                    sp.wait_ge(weighed, NC * (2 * m + u - 1))
                    sp.wait_ge(xb_ready, 2 * m + u - 1)
                sp.dma_start(adj[:, u, :], adj_rows[bass.ds((2 * m + u) * P, P), :]).then_inc(adj_loaded[u], 16)
                sp.dma_start(xres[:, u, :], x_rows[bass.ds((2 * m + u) * P, P), :]) \
                    .then_inc(xres_loaded[u], 16)

            def late(m, u):
                front(m, u)
                norm.store(sp, out_rows, *before(*before(m, u)))

            front(0, 0)
            front(0, 1)
            pairs(sp, 2, T, late)
            norm.store(sp, out_rows, T // 2 - 1, 0)
            norm.store(sp, out_rows, T // 2 - 1, 1)
            norm.all_stored(sp)

        @block.gpsimd
        def _(pool):
            norm.exponent(nc, pool)
            pairs(pool, 0, T, lambda m, u: norm.deviation(nc, pool, 2 * m + u))

        @block.tensor
        def _(pe):
            def front(m, u):
                t = 2 * m + u
                for c, (lo, width) in enumerate(CHUNKS):
                    n, slot = NC * t + c, (NC * u + c) % 2
                    if not (isinstance(n, int) and n < 2):
                        pe.wait_ge(slot_free, n - 1)
                    banks = [(z, min(BANK, width - z)) for z in range(0, width, BANK)]
                    terms = [(a, b, j) for j in range(J) for a, b in ((0, 0), (0, 1), (1, 0))]
                    for k, (a, b, j) in enumerate(terms):
                        for z, w in banks:
                            mm = nc.tensor.matmul(slots[:, slot, z:z + w], ht[a][:, j, bass.ds(t * P, P)],
                                                  ht[b][:, j, lo + z:lo + z + w],
                                                  start=k == 0, stop=k == len(terms) - 1)
                    mm.then_inc(slot_full, 1)

            def back(m, u):
                t = 2 * m + u

                def turn(g):
                    n = NG * t + g
                    if g % 2 == 0:
                        pe.wait_ge(weighed, NC * t + g // 2 + 1)
                    if not (isinstance(n, int) and n < 2):
                        pe.wait_ge(pt_low, n - 1)
                    for k in GROUPS[g]:
                        r = rows_of(k)
                        mm = nc.tensor.transpose(ps_t[0:r, g % 2, (k % GB) * P:(k % GB + 1) * P],
                                                 sc[:, u, k * P:k * P + r], ident[:, :])
                    mm.then_inc(turned, 1)

                def multiply(g):
                    pe.wait_ge(pt_low, NG * t + g + 1)
                    if g == 0 and not (isinstance(m, int) and m == 0):
                        pe.wait_ge(r_ready, t - 1)
                    for k in GROUPS[g]:
                        r = rows_of(k)
                        for a, b in ((0, 0), (0, 1), (1, 0)):
                            mm = nc.tensor.matmul(
                                ps_o[:, u, :], pt[a][0:r, g % 2, (k % GB) * P:(k % GB + 1) * P],
                                sup[b][0:r, k, :], start=k == 0 and a + b == 0,
                                stop=k == T - 1 and a == 1)
                    mm.then_inc(used, 1)

                turn(0)
                for g in range(1, NG):
                    turn(g)
                    multiply(g - 1)
                multiply(NG - 1)

            tiles(pe, front, back)

        @block.scalar
        def _(act):
            def exps(m, u):
                t = 2 * m + u
                act.wait_ge(nmax_ready, t + 1)
                if not (isinstance(m, int) and m == 0):
                    act.wait_ge(ssum_ready, t - 1)
                for c, (lo, width) in enumerate(CHUNKS):
                    nc.scalar.activation(sc[:, u, lo:lo + width], sc[:, u, lo:lo + width], ACT.Exp,
                                         bias=nmax[:, :], accum_out=esum[:, u, c:c + 1]).then_inc(exp_done, 1)

            def highs(m, u):
                for g in range(NG):
                    n = NG * (2 * m + u) + g
                    act.wait_ge(turned, n + 1)
                    if not (isinstance(n, int) and n < 2):
                        act.wait_ge(used, n - 1)
                    w = P * len(GROUPS[g])
                    nc.scalar.activation(pt[0][:, g % 2, 0:w], ps_t[:, g % 2, 0:w], ACT.Copy, scale=P_S) \
                        .then_inc(pt_high, 1)

            def both(m, u):
                highs(*before(m, u))
                exps(m, u)

            exps(0, 0)
            both(0, 1)
            both(1, 0)
            both(1, 1)
            pairs(act, 4, T, both)
            highs(T // 2 - 1, 1)

        @block.vector
        def _(dve):
            def prepare(m, u):
                t = 2 * m + u
                dve.wait_ge(adj_loaded[u], 16 * m + 16)
                nc.vector.tensor_scalar(out=bias[:, :], in0=adj[:, u, :], scalar1=0.0, scalar2=BIG2 * Q_S * Q_S,
                                        op0=ALU.is_le, op1=ALU.mult).then_inc(bias_ready, 1)
                nc.vector.tensor_reduce(out=degree[:, bass.ds(t, 1)], in_=adj[:, u, :], axis=AX.X, op=ALU.add) \
                    .then_inc(degree_ready, 1)
                dve.wait_ge(xres_loaded[u], 16 * m + 16)
                nc.vector.tensor_tensor(out=xb[:, u, :], in0=xres[:, u, :], in1=bias_row[:, :], op=ALU.add) \
                    .then_inc(xb_ready, 1)

            def mask(m, u):
                t = 2 * m + u
                dve.wait_ge(bias_ready, t + 1)
                for c, (lo, width) in enumerate(CHUNKS):
                    wait_apart(dve, slot_full, NC * t + c + 1, norm.power_ready)
                    nc.vector.tensor_tensor_reduce(
                        out=sc[:, u, lo:lo + width], in0=slots[:, (NC * u + c) % 2, 0:width],
                        in1=bias[:, lo:lo + width], scale=1.0 / (Q_S * Q_S), scalar=-3.0e38,
                        op0=ALU.add, op1=ALU.max, accum_out=mx[:, c:c + 1]).then_inc(slot_free, 1)
                dve.wait_ge(slot_free, NC * (t + 1))
                if not is_tile(m, u, 0):
                    dve.wait_ge(exp_done, NC * t)
                nc.vector.tensor_reduce(out=nmax[:, :], in_=mx[:, :], axis=AX.X, op=ALU.max, negate=True) \
                    .then_inc(nmax_ready, 1)

            def weigh(m, u):
                t = 2 * m + u
                for c, (lo, width) in enumerate(CHUNKS):
                    dve.wait_ge(exp_done, NC * t + c + 1)
                    nc.vector.tensor_tensor(out=sc[:, u, lo:lo + width], in0=sc[:, u, lo:lo + width],
                                            in1=adj[:, u, lo:lo + width], op=ALU.mult).then_inc(weighed, 1)
                nc.vector.tensor_reduce(out=ssum[:, :], in_=esum[:, u, :], axis=AX.X, op=ALU.add) \
                    .then_inc(ssum_ready, 1)
                dve.wait_ge(ssum_ready, t + 1)
                nc.vector.reciprocal(rinv[:, :], ssum[:, :]).then_inc(rinv_ready, 1)
                dve.wait_ge(rinv_ready, t + 1)
                nc.vector.scalar_tensor_tensor(out=rscale[:, u:u + 1], in0=rinv[:, :], scalar=1.0 / (P_S * V_S),
                                               in1=natt[:, bass.ds(t, 1)], op0=ALU.mult, op1=ALU.mult) \
                    .then_inc(rscale_ready, 1)

            def back(m, u):
                t = 2 * m + u
                for g in range(NG):
                    dve.wait_ge(pt_high, NG * t + g + 1)
                    w = P * len(GROUPS[g])
                    nc.vector.scalar_tensor_tensor(
                        out=pt[1][:, g % 2, 0:w], in0=ps_t[:, g % 2, 0:w], scalar=P_S,
                        in1=pt[0][:, g % 2, 0:w], op0=ALU.mult, op1=ALU.subtract).then_inc(pt_low, 1)
                dve.wait_ge(used, NG * (t + 1))
                dve.wait_ge(rscale_ready, t + 1)
                nc.vector.scalar_tensor_tensor(out=norm.r[:, :], in0=ps_o[:, u, :], scalar=rscale[:, u:u + 1],
                                               in1=xb[:, u, :], op0=ALU.mult, op1=ALU.add).then_inc(r_ready, 1)
                dve.wait_ge(r_ready, t + 1)
                norm.statistics(nc, dve, t)
                norm.finish(nc, dve, m, u)

            def step(m, u):
                mask(m, u)
                back(*before(m, u))
                weigh(m, u)

            def both(m, u):
                step(m, u)
                prepare(*after(m, u))

            prepare(0, 0)
            mask(0, 0)
            weigh(0, 0)
            prepare(0, 1)
            pairs(dve, 1, T - 1, both)
            step(T // 2 - 1, 1)
            back(T // 2 - 1, 1)


def node_attention(nc, z, natt):
    with ExitStack() as ctx:
        s = Scope(nc, ctx, "node")
        m1, m2, nm = s.sb("m1", [P, 1]), s.sb("m2", [P, 1]), s.sb("nm", [P, 1])
        e, s1, s2, r = s.sb("e", [P, T]), s.sb("s1", [P, 1]), s.sb("s2", [P, 1]), s.sb("r", [P, 1])
        row_max, all_max = s.sem("row_max"), s.sem("all_max")
        neg_max, exps = s.sem("neg_max"), s.sem("exps")
        all_sum, recip, done = s.sem("all_sum"), s.sem("recip"), s.sem("done")
        block = ctx.enter_context(nc.Block())

        @block.gpsimd
        def _(pool):
            pool.wait_ge(row_max, 1)
            nc.gpsimd.partition_all_reduce(m2[:, :], m1[:, :], P, bass.bass_isa.ReduceOp.max) \
                .then_inc(all_max, 1)
            pool.wait_ge(exps, 1)
            nc.gpsimd.partition_all_reduce(s2[:, :], s1[:, :], P, bass.bass_isa.ReduceOp.add) \
                .then_inc(all_sum, 1)

        @block.scalar
        def _(act):
            act.wait_ge(all_max, 1)
            nc.scalar.mul(nm[:, :], m2[:, :], -1.0).then_inc(neg_max, 1)
            act.wait_ge(neg_max, 1)
            nc.scalar.activation(e[:, :], z[:, :], ACT.Exp, bias=nm[:, :], accum_out=s1[:, :]).then_inc(exps, 1)

        @block.vector
        def _(dve):
            nc.vector.tensor_reduce(out=m1[:, :], in_=z[:, :], axis=AX.X, op=ALU.max).then_inc(row_max, 1)
            dve.wait_ge(all_sum, 1)
            nc.vector.reciprocal(r[:, :], s2[:, :]).then_inc(recip, 1)
            dve.wait_ge(recip, 1)
            nc.vector.tensor_scalar(out=natt[:, :], in0=e[:, :], scalar1=r[:, :], scalar2=None, op0=ALU.mult) \
                .then_inc(done, 1)


def aggregate(nc, tag, x_rows, out_rows, adj_cols, y, bias_row, ident, dcol=None):
    with ExitStack() as ctx:
        s = Scope(nc, ctx, tag)
        a32 = s.sb("adj32", [P, 2, T, P])
        a16 = s.sb("adj16", [P, 2, T, P], F16)
        xres = s.sb("xres", [P, 2, D])
        act_in = s.sb("act_in", [P, D])
        norm = Norm(s)
        ps = s.ps("ps", [P, 2, BANK])
        adj_loaded = [s.sem(f"adj_loaded{u}") for u in range(2)]
        xres_loaded = [s.sem(f"xres_loaded{u}") for u in range(2)]
        narrowed = s.sem("narrowed")
        diag_ready = s.sem("diag_ready")
        summed = s.sem("summed")
        biased = s.sem("biased")
        r_ready = s.sem("r_ready")
        block = ctx.enter_context(nc.Block())

        @block.sync
        def _(sp):
            def load(m, u):
                t = 2 * m + u
                if not (isinstance(m, int) and m == 0):
                    sp.wait_ge(narrowed, t - 1)
                    sp.wait_ge(r_ready, t - 1)
                sp.dma_start(a32[:, u, :, :], adj_cols[bass.ds(t, 1), :, :, :].rearrange("o p k q -> (o p) k q")) \
                    .then_inc(adj_loaded[u], 16)
                sp.dma_start(xres[:, u, :], x_rows[bass.ds(t * P, P), :]).then_inc(xres_loaded[u], 16)

            def late(m, u):
                load(m, u)
                norm.store(sp, out_rows, *before(*before(m, u)))

            load(0, 0)
            load(0, 1)
            pairs(sp, 2, T, late)
            norm.store(sp, out_rows, T // 2 - 1, 0)
            norm.store(sp, out_rows, T // 2 - 1, 1)
            norm.all_stored(sp)

        @block.gpsimd
        def _(pool):
            norm.exponent(nc, pool)
            pairs(pool, 0, T, lambda m, u: norm.deviation(nc, pool, 2 * m + u))

        @block.scalar
        def _(act):
            def step(m, u):
                act.wait_ge(adj_loaded[u], 16 * m + 16)
                if not (isinstance(m, int) and m == 0):
                    act.wait_ge(summed, 2 * m + u - 1)
                nc.scalar.activation(a16[:, u, :, :], a32[:, u, :, :], ACT.Copy).then_inc(narrowed, 1)

            step(0, 0)
            step(0, 1)
            pairs(act, 2, T, step)

        @block.tensor
        def _(pe):
            def step(m, u):
                t = 2 * m + u
                pe.wait_ge(narrowed if dcol is None else diag_ready, t + 1)
                if not (isinstance(m, int) and m == 0):
                    pe.wait_ge(biased, t - 1)
                for k in range(T):
                    r = rows_of(k)
                    for b in range(2):
                        mm = nc.tensor.matmul(ps[:, u, :], a16[0:r, u, k, :], y[b][0:r, k, :],
                                              start=k == 0 and b == 0, stop=k == T - 1 and b == 1)
                mm.then_inc(summed, 1)

            step(0, 0)
            step(0, 1)
            pairs(pe, 2, T, step)

        @block.vector
        def _(dve):
            def identity(m, u):
                t = 2 * m + u
                dve.wait_ge(narrowed, t + 1)
                part = a16[:, u, bass.ds(t, 1), :].rearrange("p o q -> p (o q)")
                nc.vector.tensor_tensor(out=part, in0=part, in1=ident[:, :], op=ALU.add).then_inc(diag_ready, 1)

            def step(m, u):
                t = 2 * m + u
                dve.wait_ge(summed, t + 1)
                scale = 1.0 / V_S if dcol is None else dcol[:, bass.ds(t, 1)]
                nc.vector.scalar_tensor_tensor(out=act_in[:, :], in0=ps[:, u, :], scalar=scale,
                                               in1=bias_row[:, :], op0=ALU.mult, op1=ALU.add).then_inc(biased, 1)
                dve.wait_ge(biased, t + 1)
                dve.wait_ge(xres_loaded[u], 16 * m + 16)
                nc.vector.scalar_tensor_tensor(out=norm.r[:, :], in0=act_in[:, :], scalar=0.0,
                                               in1=xres[:, u, :], op0=ALU.max, op1=ALU.add).then_inc(r_ready, 1)
                dve.wait_ge(r_ready, t + 1)
                norm.statistics(nc, dve, t)
                norm.finish(nc, dve, m, u)

            if dcol is None:
                pairs(dve, 0, T, step)
            else:
                def both(m, u):
                    identity(*after(m, u))
                    step(m, u)

                identity(0, 0)
                pairs(dve, 0, T - 1, both)
                step(T // 2 - 1, 1)


def degree_scales(nc, degree, dy, dout):
    with ExitStack() as ctx:
        s = Scope(nc, ctx, "degree")
        d1, d, power = s.sb("d1", [P, T]), s.sb("d", [P, T]), s.sb("power", [P, T])
        d1_ready, d_ready = s.sem("d1_ready"), s.sem("d_ready")
        block = ctx.enter_context(nc.Block())

        @block.gpsimd
        def _(pool):
            nc.gpsimd.memset(power[:, :], -0.5).then_inc(d1_ready, 1)
            nc.gpsimd.tensor_scalar(out=d1[:, :], in0=degree[:, :], scalar1=1.0, scalar2=1.0, op0=ALU.mult,
                                    op1=ALU.add).then_inc(d1_ready, 1)
            pool.wait_ge(d1_ready, 2)
            nc.gpsimd.tensor_tensor(out=d[:, :], in0=d1[:, :], in1=power[:, :], op=ALU.pow).then_inc(d_ready, 1)

        @block.vector
        def _(dve):
            dve.wait_ge(d_ready, 1)
            nc.vector.tensor_scalar(out=dy[:, :], in0=d[:, :], scalar1=V_S * XW, scalar2=None, op0=ALU.mult)
            nc.vector.tensor_scalar(out=dout[:, :], in0=d[:, :], scalar1=1.0 / V_S, scalar2=None, op0=ALU.mult)


def build(nc, x, adj, adj_cols, wk, wq, wv, wo, w1, b1, w2, b2, node_w, edge_w, w3, b3, out, stop=99):
    x1, x2, x3 = (nc.dram_tensor(f"x{n}", [NP, D], F32).ap() for n in (1, 2, 3))
    with ExitStack() as outer:
        g = Scope(nc, outer, "all")
        ident = g.sb("ident", [P, P])
        rows = {name: g.sb(name, [P, D]) for name in ("b1_row", "b2_row", "b3_row", "node_row")}
        z, natt, degree = g.sb("z", [P, T]), g.sb("natt", [P, T]), g.sb("degree", [P, T])
        dy, dout = g.sb("dy", [P, T]), g.sb("dout", [P, T])
        cleared, made, loaded = g.sem("cleared"), g.sem("made"), g.sem("loaded")
        with nc.Block() as block:
            @block.gpsimd
            def _(pool):
                nc.gpsimd.memset(ident[:, :], 0.0).then_inc(cleared, 1)
                nc.gpsimd.memset(z[:, :], -3.0e38).then_inc(made, 1)
                pool.wait_ge(cleared, 1)
                nc.gpsimd.affine_select(out=ident[:, :], in_=ident[:, :], compare_op=ALU.not_equal, fill=1.0,
                                        base=0, pattern=[[-1, P]], channel_multiplier=1).then_inc(made, 1)

            @block.sync
            def _(sp):
                for name, src in (("b1_row", b1), ("b2_row", b2), ("b3_row", b3), ("node_row", node_w)):
                    sp.dma_start(rows[name][:, :], src.broadcast_to([P, D])).then_inc(loaded, 16)
                sp.wait_ge(loaded, 64)

        with ExitStack() as ctx:
            s = Scope(nc, ctx, "l0")
            kk = s.sb("kk", [P, H, NP], F16)
            vv = s.sb("vv", [P, T, H, P], F16)
            with ExitStack() as inner:
                w = Scope(nc, inner, "l0w")
                wkh, wkl, wvh, wvl = (w.sb(n, [P, J, D], F16) for n in ("wkh", "wkl", "wvh", "wvl"))
                weights_phase(nc, "w0", [(wk, wkh[:, :, :], wkl[:, :, :]), (wv, wvh[:, :, :], wvl[:, :, :])])

                def keys(t, bank):
                    part = bank.rearrange("p (c r) -> p c r", c=J)
                    return [(part[KD * e:KD * e + KD, :, :], kk[0:KD, e::2, bass.ds(t * P, P)],
                             kk[KD:P, e::2, bass.ds(t * P, P)], Q_S * XW) for e in range(2)]

                def values(t, bank):
                    part = bank.rearrange("p (h k) -> p h k", h=H)
                    dst = vv[:, bass.ds(t, 1), :, :].rearrange("p o h k -> p (o h) k")
                    return [(part, dst[:, :, 0:KD], dst[:, :, KD:P], V_S * XW)]

                project(nc, "p0", x, ident, [("cols", wkh, wkl, keys), ("rows", wvh, wvl, values)])
            wqd = [s.sb(f"wqd{a}", [P, J, H * P], F16) for a in range(2)]
            woh = [s.sb(f"wo{a}", [P, J, D], F16) for a in range(2)]
            weights_phase(nc, "w0q", [(wq, wqd[0][:, :, :], wqd[1][:, :, :])])
            weights_phase(nc, "w0o", [(wo, woh[0][:, :, :], woh[1][:, :, :])])
            attention(nc, x, x1, adj, kk, vv, wqd, woh, ident)
        if stop == 0:
            return x1

        def split_rows(y):
            return lambda t, bank: [(bank, y[0][:, bass.ds(t, 1), :].rearrange("p o n -> p (o n)"),
                                     y[1][:, bass.ds(t, 1), :].rearrange("p o n -> p (o n)"), V_S * XW)]

        with ExitStack() as ctx:
            s = Scope(nc, ctx, "l1")
            y = [s.sb(f"y{a}", [P, T, D], F16) for a in range(2)]
            w = [s.sb(f"w{a}", [P, J, D], F16) for a in range(2)]
            weights_phase(nc, "w1", [(w1, w[0][:, :, :], w[1][:, :, :])])
            project(nc, "p1", x1, ident, [("rows", w[0], w[1], split_rows(y))])
            aggregate(nc, "a1", x1, x2, adj_cols, y, rows["b1_row"], ident)
        if stop == 1:
            return x2

        with ExitStack() as ctx:
            s = Scope(nc, ctx, "l2")
            ht = [s.sb(f"ht{a}", [P, J, NP], F16) for a in range(2)]
            sup = [s.sb(f"sup{a}", [P, T, D], F16) for a in range(2)]
            with ExitStack() as inner:
                w = Scope(nc, inner, "l2w")
                weh, wel, wsh, wsl = (w.sb(n, [P, J, D], F16) for n in ("weh", "wel", "wsh", "wsl"))
                weights_phase(nc, "w2", [(edge_w, weh[:, :, :], wel[:, :, :]), (w2, wsh[:, :, :], wsl[:, :, :])])

                def columns(t, bank):
                    return [(bank.rearrange("p (c r) -> p c r", c=J), ht[0][:, :, bass.ds(t * P, P)],
                             ht[1][:, :, bass.ds(t * P, P)], Q_S * XW)]

                project(nc, "p2", x2, ident, [("cols", weh, wel, columns), ("rows", wsh, wsl, split_rows(sup))],
                        score=(rows["node_row"], z))
            node_attention(nc, z, natt)
            edge_attention(nc, x2, x3, adj, ht, sup, natt, rows["b2_row"], degree, ident)
        if stop == 2:
            return x3

        with ExitStack() as ctx:
            s = Scope(nc, ctx, "l3")
            y = [s.sb(f"y{a}", [P, T, D], F16) for a in range(2)]
            w = [s.sb(f"w{a}", [P, J, D], F16) for a in range(2)]
            degree_scales(nc, degree, dy, dout)
            weights_phase(nc, "w3", [(w3, w[0][:, :, :], w[1][:, :, :])])
            project(nc, "p3", x3, ident, [("rows", w[0], w[1], split_rows(y))], row_scale=dy)
            aggregate(nc, "a3", x3, out, adj_cols, y, rows["b3_row"], ident, dcol=dout)


def kernel(x, adj, L0_gnn_Wks, L0_gnn_Wqs, L0_gnn_Wvs, L0_gnn_Wo, L1_gnn_W, L1_gnn_b, L2_gnn_weight,
           L2_gnn_bias, L2_gnn_node_w, L2_gnn_edge_w, L3_gnn_W, L3_gnn_b):
    import concourse.bacc as bacc
    from concourse.bass_utils import run_bass_kernel_spmd

    def heads(w, times=1):
        w = np.asarray(w).transpose(1, 0, 2)
        return np.concatenate([w] * times, axis=2).reshape(D, -1)

    def padded(a, shape):
        out = np.zeros(shape, np.float32)
        out[:a.shape[0], :a.shape[1]] = a
        return out

    x, adj = np.asarray(x), np.asarray(adj)
    cols = padded(adj.T, (NP, NP)).reshape(T, P, T, P).transpose(2, 1, 0, 3)
    arrays = {
        "x": padded(x, (NP, D)), "adj": padded(adj, (NP, N)), "adj_cols": cols,
        "wk": heads(L0_gnn_Wks), "wq": heads(L0_gnn_Wqs, 2), "wv": heads(L0_gnn_Wvs),
        "wo": np.asarray(L0_gnn_Wo).reshape(H * KD, D),
        "w1": np.asarray(L1_gnn_W).T, "b1": np.asarray(L1_gnn_b).reshape(1, D),
        "w2": np.asarray(L2_gnn_weight), "b2": np.asarray(L2_gnn_bias).reshape(1, D),
        "node_w": np.asarray(L2_gnn_node_w).reshape(1, D), "edge_w": np.asarray(L2_gnn_edge_w),
        "w3": np.asarray(L3_gnn_W).T, "b3": np.asarray(L3_gnn_b).reshape(1, D),
    }
    arrays = {k: np.ascontiguousarray(v) for k, v in arrays.items()}
    nc = bacc.Bacc("TRN2", target_bir_lowering=False, num_devices=1)
    args = {k: nc.dram_tensor(f"in_{k}", v.shape, F32, kind="ExternalInput").ap() for k, v in arrays.items()}
    out = nc.dram_tensor("out_rows", (NP, D), F32, kind="ExternalOutput").ap()
    build(nc, **args, out=out)
    result = run_bass_kernel_spmd(nc, [{f"in_{k}": v for k, v in arrays.items()}], core_ids=[0])
    return result.results[0]["out_rows"][:N]
```

```python
from contextlib import ExitStack

import numpy as np

import concourse.bass as bass
from concourse import mybir

F32 = mybir.dt.float32
F16 = mybir.dt.float16
ALU = mybir.AluOpType
ACT = mybir.ActivationFunctionType
AX = mybir.AxisListType

P = 128
N = 2708
D = 512
H = 8
KD = 64
T = -(-N // P)
NP = T * P
LAST = N - (T - 1) * P
J = D // P
BANK = 512
CHUNK = 2 * BANK
CHUNKS = [(c, min(CHUNK, N - c)) for c in range(0, N, CHUNK)]
NC = len(CHUNKS)
GB = BANK // P
GROUPS = [list(range(g, min(g + GB, T))) for g in range(0, T, GB)]
NG = len(GROUPS)
assert NG == 2 * NC and T % 2 == 0 and N % P

X_S, W_S, Q_S, V_S, P_S, O_S = 16.0, 256.0, 16.0, 16.0, 1024.0, 16.0
XW = 1.0 / (X_S * W_S)
EPS = 1e-5
BIG0 = 1e16
BIG2 = -9000000000000000.0


def wait_apart(eng, sem, value, met):
    if not isinstance(value, int):
        value = eng.to_reg(value)
    eng.wait_ge(met, 1)
    eng.wait_ge(sem, value)


def rows_of(k):
    return P if k < T - 1 else LAST


class Scope:

    def __init__(self, nc, ctx, tag):
        self.nc, self.ctx, self.tag, self.sems = nc, ctx, tag, []
        ctx.callback(self.release)

    def release(self):
        if self.sems:
            self.nc.clear_and_free_semaphores(self.sems)
            self.nc.all_engine_barrier()

    def sb(self, name, shape, dt=F32):
        return self.ctx.enter_context(self.nc.sbuf_tensor(f"{self.tag}_{name}", shape, dt))

    def ps(self, name, shape):
        return self.ctx.enter_context(self.nc.psum_tensor(f"{self.tag}_{name}", shape, F32))

    def sem(self, name):
        self.sems.append(self.nc.alloc_semaphore(f"{self.tag}_{name}"))
        return self.sems[-1]


def product3(nc, out, lhs, rhs, first=True, last=True):
    terms = [(a, b, j) for j in range(J) for a, b in ((0, 0), (0, 1), (1, 0))]
    for n, (a, b, j) in enumerate(terms):
        mm = nc.tensor.matmul(out, lhs(a, j), rhs(b, j), start=first and n == 0,
                              stop=last and n == len(terms) - 1)
    return mm


def split_weights(nc, s, block, jobs):
    loaded, high, low = s.sem("w_loaded"), s.sem("w_high"), s.sem("w_low")

    @block.sync
    def _(sp):
        for src, _h, _l, stage in jobs:
            sp.dma_start(stage, src).then_inc(loaded, 16)

    @block.scalar
    def _(act):
        act.wait_ge(loaded, 16 * len(jobs))
        for _src, h, _l, stage in jobs:
            nc.scalar.activation(h, stage, ACT.Copy, scale=W_S).then_inc(high, 1)

    @block.vector
    def _(dve):
        for n, (_src, h, l, stage) in enumerate(jobs):
            dve.wait_ge(high, n + 1)
            nc.vector.scalar_tensor_tensor(out=l, in0=stage, scalar=W_S, in1=h, op0=ALU.mult,
                                           op1=ALU.subtract).then_inc(low, 1)


def weights_phase(nc, tag, specs):
    with ExitStack() as ctx:
        s = Scope(nc, ctx, tag)
        jobs = []
        for n, (src, h, l) in enumerate(specs):
            stage = s.sb(f"stage{n}", [P, J, src.shape[1]])
            jobs.append((src.rearrange("(j p) n -> p j n", p=P), h, l, stage[:, :, :]))
        block = ctx.enter_context(nc.Block())
        split_weights(nc, s, block, jobs)


def pairs(eng, begin, end, step):
    turns = (end - begin) // 2
    with eng.Fori(0, turns) as i:
        for t in (begin, begin + 1):
            step(i + t // 2, t % 2)
    if (end - begin) % 2:
        step((end - 1) // 2, (end - 1) % 2)


def after(m, u):
    return (m, 1) if u == 0 else (m + 1, 0)


def project(nc, tag, x_rows, ident, jobs, score=None, row_scale=None):
    with ExitStack() as ctx:
        s = Scope(nc, ctx, tag)
        x_in = s.sb("x_in", [P, 2, D])
        xt = s.sb("xt", [P, 2, 2, J, P], F16)
        junk = s.sb("junk", [P, D])
        ps_t = s.ps("ps_t", [P, 2, BANK])
        ps_job = [s.ps(f"ps_job{n}", [P, 2, BANK]) for n in range(len(jobs))]
        x_loaded = [s.sem(f"x_loaded{u}") for u in range(2)]
        turned = s.sem("turned")
        xt_high = s.sem("xt_high")
        xt_low = s.sem("xt_low")
        made = s.sem("made")
        out_high = s.sem("out_high")
        out_low = s.sem("out_low")
        weighed = s.sem("weighed")
        scored = s.sem("scored")
        nj = len(jobs)
        block = ctx.enter_context(nc.Block())

        @block.sync
        def _(sp):
            def load(m, u):
                if not (isinstance(m, int) and m == 0):
                    sp.wait_ge(turned, 2 * m + u - 1)
                    if score is not None:
                        sp.wait_ge(scored, 2 * m + u - 1)
                sp.dma_start(x_in[:, u, :], x_rows[bass.ds((2 * m + u) * P, P), :]) \
                    .then_inc(x_loaded[u], 16)

            load(0, 0)
            load(0, 1)
            pairs(sp, 2, T, load)

        @block.tensor
        def _(pe):
            def turn(m, u):
                pe.wait_ge(x_loaded[u], 16 * m + 16)
                if not (isinstance(m, int) and m == 0):
                    pe.wait_ge(xt_low, 2 * m + u - 1)
                for j in range(J):
                    mm = nc.tensor.transpose(ps_t[:, u, j * P:(j + 1) * P],
                                             x_in[:, u, j * P:(j + 1) * P], ident[:, :])
                mm.then_inc(turned, 1)

            def multiply(m, u):
                pe.wait_ge(xt_low, 2 * m + u + 1)
                for n, (kind, wh, wl, _) in enumerate(jobs):
                    w = (wh, wl)
                    if not (isinstance(m, int) and m == 0):
                        pe.wait_ge(out_low, nj * (2 * m + u - 2) + n + 1)
                    if kind == "rows":
                        mm = product3(nc, ps_job[n][:, u, :], lambda a, j: xt[:, u, a, j, :],
                                      lambda b, j: w[b][:, j, :])
                    else:
                        for c in range(J):
                            mm = product3(nc, ps_job[n][:, u, c * P:(c + 1) * P],
                                          lambda a, j: w[a][:, j, c * P:(c + 1) * P],
                                          lambda b, j: xt[:, u, b, j, :])
                    mm.then_inc(made, 1)

            def step(m, u):
                turn(*after(m, u))
                multiply(m, u)

            turn(0, 0)
            step(0, 0)
            step(0, 1)
            pairs(pe, 2, T - 1, step)
            multiply(T // 2 - 1, 1)

        @block.scalar
        def _(act):
            def split(m, u):
                act.wait_ge(turned, 2 * m + u + 1)
                if not (isinstance(m, int) and m == 0):
                    act.wait_ge(made, nj * (2 * m + u - 1))
                nc.scalar.activation(xt[:, u, 0, :, :], ps_t[:, u, :].rearrange("p (j r) -> p j r", j=J),
                                     ACT.Copy, scale=X_S).then_inc(xt_high, 1)

            def finish(m, u):
                t = 2 * m + u
                for n, (_, _, _, pieces) in enumerate(jobs):
                    act.wait_ge(made, nj * t + n + 1)
                    for part, high, _low, scale in pieces(t, ps_job[n][:, u, :]):
                        if row_scale is not None:
                            scale = row_scale[:, bass.ds(t, 1)]
                        op = nc.scalar.activation(high, part, ACT.Copy, scale=scale)
                    op.then_inc(out_high, 1)

            def step(m, u):
                split(*after(m, u))
                finish(m, u)

            split(0, 0)
            step(0, 0)
            pairs(act, 1, T - 1, step)
            finish(T // 2 - 1, 1)

        @block.vector
        def _(dve):
            def split(m, u):
                t = 2 * m + u
                dve.wait_ge(xt_high, t + 1)
                nc.vector.scalar_tensor_tensor(
                    out=xt[:, u, 1, :, :], in0=ps_t[:, u, :].rearrange("p (j r) -> p j r", j=J), scalar=X_S,
                    in1=xt[:, u, 0, :, :], op0=ALU.mult, op1=ALU.subtract).then_inc(xt_low, 1)
                if score is not None:
                    node_w, z = score
                    r = LAST if isinstance(m, int) and t == T - 1 else P
                    dve.wait_ge(x_loaded[u], 16 * m + 16)
                    if not (isinstance(m, int) and t == 0):
                        dve.wait_ge(scored, t)
                    nc.vector.tensor_tensor(out=junk[0:r, :], in0=x_in[0:r, u, :], in1=node_w[0:r, :],
                                            op=ALU.mult).then_inc(weighed, 1)
                    dve.wait_ge(weighed, t + 1)
                    nc.vector.tensor_reduce(out=z[0:r, bass.ds(t, 1)], in_=junk[0:r, :], axis=AX.X,
                                            op=ALU.add).then_inc(scored, 1)

            def finish(m, u):
                t = 2 * m + u
                for n, (_, _, _, pieces) in enumerate(jobs):
                    dve.wait_ge(out_high, nj * t + n + 1)
                    for part, high, low, scale in pieces(t, ps_job[n][:, u, :]):
                        if row_scale is not None:
                            scale = row_scale[:, bass.ds(t, 1)]
                        op = nc.vector.scalar_tensor_tensor(out=low, in0=part, scalar=scale, in1=high,
                                                            op0=ALU.mult, op1=ALU.subtract)
                    op.then_inc(out_low, 1)

            def step(m, u):
                split(*after(m, u))
                finish(m, u)

            split(0, 0)
            step(0, 0)
            pairs(dve, 1, T - 3, step)
            for t in range(T - 3, T - 1):
                step(t // 2, t % 2)
            finish(T // 2 - 1, 1)


def before(m, u):
    return (m, 0) if u == 1 else (m - 1, 1)


def is_tile(m, u, t):
    return isinstance(m, int) and 2 * m + u == t


class Norm:

    def __init__(self, s):
        self.r = s.sb("residual", [P, D])
        self.stats, self.mv = s.sb("stats", [P, 6]), s.sb("mv", [P, 2])
        self.veps, self.rstd = s.sb("veps", [P, 1]), s.sb("rstd", [P, 1])
        self.power = s.sb("power", [P, 1])
        self.out = s.sb("x_out", [P, 2, D])
        self.stats_ready = s.sem("stats_ready")
        self.mv_ready = s.sem("mv_ready")
        self.power_ready = s.sem("power_ready")
        self.veps_ready = s.sem("veps_ready")
        self.rstd_ready = s.sem("rstd_ready")
        self.x_ready = s.sem("x_ready")
        self.stored = [s.sem(f"x_stored{u}") for u in range(2)]

    def statistics(self, nc, dve, t):
        nc.vector.bn_stats(out=self.stats[:, :], in_=self.r[:, :]).then_inc(self.stats_ready, 1)
        wait_apart(dve, self.stats_ready, t + 1, self.power_ready)
        nc.vector.bn_aggr(out=self.mv[:, :], in_=self.stats[:, :]).then_inc(self.mv_ready, 1)

    def exponent(self, nc, pool):
        nc.gpsimd.memset(self.power[:, :], -0.5).then_inc(self.power_ready, 1)
        pool.wait_ge(self.power_ready, 1)

    def deviation(self, nc, pool, t):
        wait_apart(pool, self.mv_ready, t + 1, self.power_ready)
        nc.gpsimd.tensor_scalar(out=self.veps[:, :], in0=self.mv[:, 1:2], scalar1=1.0, scalar2=EPS,
                                op0=ALU.mult, op1=ALU.add).then_inc(self.veps_ready, 1)
        pool.wait_ge(self.veps_ready, t + 1)
        nc.gpsimd.tensor_tensor(out=self.rstd[:, :], in0=self.veps[:, :], in1=self.power[:, :],
                                op=ALU.pow).then_inc(self.rstd_ready, 1)

    def finish(self, nc, dve, m, u):
        dve.wait_ge(self.rstd_ready, 2 * m + u + 1)
        if not (isinstance(m, int) and m == 0):
            dve.wait_ge(self.stored[u], 16 * m)
        nc.vector.tensor_scalar(out=self.out[:, u, :], in0=self.r[:, :], scalar1=self.mv[:, 0:1],
                                scalar2=self.rstd[:, :], op0=ALU.subtract, op1=ALU.mult) \
            .then_inc(self.x_ready, 1)

    def store(self, sp, rows, m, u):
        sp.wait_ge(self.x_ready, 2 * m + u + 1)
        sp.dma_start(rows[bass.ds((2 * m + u) * P, P), :], self.out[:, u, :]).then_inc(self.stored[u], 16)

    def all_stored(self, sp):
        for u in range(2):
            sp.wait_ge(self.stored[u], 16 * (T // 2))


def attention(nc, x_rows, out_rows, adj_rows, kk, vv, wq, wo, ident):
    with ExitStack() as ctx:
        s = Scope(nc, ctx, "att")
        adj = s.sb("adj", [P, 2, NP])
        xq = s.sb("xq", [P, D])
        xres = s.sb("xres", [P, 2, D])
        xt = s.sb("xt", [P, 2, J, P], F16)
        q_raw = s.sb("q_raw", [P, 2, J, P], F16)
        q = s.sb("q", [P, 2, 2, 2, J, P], F16)
        sp_sb = s.sb("scores", [P, 2, N])
        pt = [s.sb(f"pt_{a}", [P, NG, BANK], F16) for a in ("high", "low")]
        o_half = s.sb("o_half", [P, 2, KD])
        o = s.sb("o", [P, 2, D])
        ot = s.sb("ot", [P, 2, J, P], F16)
        mx, nmax = s.sb("mx", [P, 2, NC]), s.sb("nmax", [P, 2])
        esum, ssum, rinv = s.sb("esum", [P, 2, NC]), s.sb("ssum", [P, 2]), s.sb("rinv", [P, 2])
        norm = Norm(s)
        slots = s.ps("slots", [P, 2, CHUNK])
        ps_t = s.ps("ps_t", [P, 2, BANK])
        ps_pv = s.ps("ps_pv", [P, 2, BANK])

        adj_loaded = [s.sem(f"adj_loaded{u}") for u in range(2)]
        xres_loaded = [s.sem(f"xres_loaded{u}") for u in range(2)]
        xq_loaded = s.sem("xq_loaded")
        q_spread = s.sem("q_spread")
        pad_clear = s.sem("pad_clear")
        diag_ready = s.sem("diag_ready")
        bias_ready = s.sem("bias_ready")
        slot_full = s.sem("slot_full")
        slot_high = s.sem("slot_high")
        slot_free = s.sem("slot_free")
        nmax_ready = s.sem("nmax_ready")
        exp_done = s.sem("exp_done")
        turned = s.sem("turned")
        pt_high = s.sem("pt_high")
        pt_low = s.sem("pt_low")
        ssum_ready = s.sem("ssum_ready")
        rinv_ready = s.sem("rinv_ready")
        pv_done = s.sem("pv_done")
        half_done = s.sem("half_done")
        o_done = s.sem("o_done")
        block = ctx.enter_context(nc.Block())

        EXTRA = {3: "ot", 4: "wo", 5: "xt", 6: "q"}
        PER_TILE = NC * H + len(EXTRA)
        assert PER_TILE % 2 == 0

        def extras(m, u):
            have = dict(EXTRA)
            if is_tile(m, u, 0):
                del have[3], have[4]
            if is_tile(m, u, T - 1):
                del have[5], have[6]
            return have

        def slots_of(m, u):
            have = extras(m, u)
            base = 2 if is_tile(m, u, 0) else 0
            place = {}
            for h in range(H):
                for use in [(h, c) for c in range(NC)] + ([have[h]] if h in have else []):
                    place[use] = (2 * m + u) * PER_TILE + base + len(place)
            return place

        def parity(m, u, use):
            place = slots_of(m, u) if isinstance(m, int) else slots_of(1, u)
            return place[use] % 2

        part_of = {"ot": (ot, O_S / (P_S * V_S)), "xt": (xt, X_S), "q": (q_raw, Q_S / 8.0 * XW)}
        TAIL = {"ot": T * PER_TILE - 2, "wo": T * PER_TILE - 1}
        HEAD = {"xt": 0, "q": 1}

        def tile_steps(m, u, step, extra):
            place = slots_of(m, u)
            for h in range(H):
                first = is_tile(m, u, 0)
                step(m, u, h, place, True, not first or h >= 1, not first or h >= 2, not first or h >= 3)
                if h in extras(m, u):
                    use = extras(m, u)[h]
                    extra(use, m, u, place[use], parity(m, u, use))

        def all_steps(eng, step, extra, around=None):
            tile = lambda m, u: tile_steps(m, u, step, extra)
            extra("xt", -1, 1, HEAD["xt"], 0)
            extra("q", -1, 1, HEAD["q"], 1)
            tile(0, 0)
            pairs(eng, 1, T - 1, tile)
            tile(T // 2 - 1, 1)
            for h, flags in enumerate([(False, True, True, True), (False, False, True, True),
                                       (False, False, False, True)]):
                step(T // 2, 0, h, None, *flags)
            extra("ot", T // 2, 0, TAIL["ot"], 0)
            extra("wo", T // 2, 0, TAIL["wo"], 1)

        @block.sync
        def _(sp):
            def spread(u, place):
                sp.wait_ge(slot_free, place + 1)
                for e in range(2):
                    for half in range(2):
                        sp.dma_start(q[half * KD:half * KD + KD, u, e, :, :, :],
                                     q_raw[e * KD:e * KD + KD, :, :, :]).then_inc(q_spread, 16)

            sp.dma_start(xq[:, :], x_rows[0:P, :]).then_inc(xq_loaded, 16)
            sp.dma_start(adj[:, 0, 0:N], adj_rows[0:P, :]).then_inc(adj_loaded[0], 16)
            spread(0, HEAD["q"])

            def tile(m, u):
                t = 2 * m + u
                if not is_tile(m, u, 0):
                    sp.wait_ge(slot_free, PER_TILE * t)
                if not is_tile(m, u, T - 1):
                    m1, u1 = after(m, u)
                    sp.dma_start(adj[:, u1, 0:N], adj_rows[bass.ds((t + 1) * P, P), :]) \
                        .then_inc(adj_loaded[u1], 16)
                    if is_tile(m, u, 0):
                        sp.wait_ge(slot_full, 1)
                    sp.dma_start(xq[:, :], x_rows[bass.ds((t + 1) * P, P), :]).then_inc(xq_loaded, 16)
                if not (isinstance(m, int) and m == 0):
                    sp.wait_ge(norm.mv_ready, t - 1)
                sp.dma_start(xres[:, u, :], x_rows[bass.ds(t * P, P), :]).then_inc(xres_loaded[u], 16)
                if not is_tile(m, u, 0):
                    norm.store(sp, out_rows, *(before(m, u)))
                if not is_tile(m, u, T - 1):
                    spread(1 - u, slots_of(m, u)["q"])

            tile(0, 0)
            pairs(sp, 1, T - 1, tile)
            tile(T // 2 - 1, 1)
            norm.store(sp, out_rows, T // 2 - 1, 1)
            norm.all_stored(sp)

        @block.gpsimd
        def _(pool):
            nc.gpsimd.memset(adj[:, :, N:NP], 0.0).then_inc(pad_clear, 1)
            norm.exponent(nc, pool)

            def bias(m, u):
                wait_apart(pool, diag_ready, 2 * m + u + 1, pad_clear)
                big = BIG0 * Q_S * Q_S
                nc.gpsimd.tensor_scalar(out=adj[:, u, 0:N], in0=adj[:, u, 0:N], scalar1=big, scalar2=-big,
                                        op0=ALU.mult, op1=ALU.add).then_inc(bias_ready, 1)

            def tile(m, u):
                if not is_tile(m, u, T - 1):
                    bias(*after(m, u))
                if not is_tile(m, u, 0):
                    norm.deviation(nc, pool, 2 * m + u - 1)

            bias(0, 0)
            tile(0, 0)
            pairs(pool, 1, T - 1, tile)
            tile(T // 2 - 1, 1)
            norm.deviation(nc, pool, T - 1)

        @block.tensor
        def _(pe):
            def values(i, h, g):
                pe.wait_ge(pt_low, NG * i + g + 1)
                b = h % 2
                for k in GROUPS[g]:
                    r = rows_of(k)
                    for a in (0, 1) if k < T - 1 else (1, 0):
                        cols = P if a == 0 else KD
                        mm = nc.tensor.matmul(ps_pv[:, b, 0:cols],
                                              pt[a][0:r, g, (k % GB) * P:(k % GB + 1) * P],
                                              vv[0:r, k, h, 0:cols], start=k == 0 and a == 0,
                                              stop=k == T - 1 and a == 0)
                return mm

            def step(m, u, h, place, scores, _exp, probs, tail):
                i = (2 * m + u) * H + h
                for c, (lo, width) in enumerate(CHUNKS):
                    if probs:
                        pe.wait_ge(exp_done, NC * (i - 2) + c + 1)
                        for g in (2 * c, 2 * c + 1):
                            n = NG * (i - 2) + g
                            if not (isinstance(n, int) and n < 2):
                                pe.wait_ge(pt_low, n - 1)
                            for k in GROUPS[g]:
                                r = rows_of(k)
                                mm = nc.tensor.transpose(ps_t[0:r, g % 2, (k % GB) * P:(k % GB + 1) * P],
                                                         sp_sb[:, h % 2, k * P:k * P + r], ident[:, :])
                            mm.then_inc(turned, 1)
                    if scores:
                        n, slot = place[h, c], parity(m, u, (h, c))
                        if c == 0 and h == 0:
                            pe.wait_ge(q_spread, 64 * (2 * m + u + 1))
                        pe.wait_ge(slot_free, n - 1)
                        for a in range(2):
                            for z in range(0, width, BANK):
                                w = min(BANK, width - z)
                                mm = nc.tensor.matmul(slots[:, slot, z:z + w], q[:, u, h % 2, a, h // 2, :],
                                                      kk[:, h, lo + z:lo + z + w],
                                                      start=a == 0, stop=a == 1)
                        mm.then_inc(slot_full, 1)
                    if c == 0:
                        if tail:
                            values(i - 3, (h - 3) % H, NG - 2)
                            values(i - 3, (h - 3) % H, NG - 1).then_inc(pv_done, 1)
                    elif probs:
                        if c == 1 and not (isinstance(i, int) and i < 4):
                            pe.wait_ge(o_done, i - 3)
                        values(i - 2, (h - 2) % H, 2 * c - 2)
                        values(i - 2, (h - 2) % H, 2 * c - 1)

            def extra(use, m, u, n, slot):
                t = 2 * m + u
                if not (isinstance(n, int) and n < 2):
                    pe.wait_ge(slot_free, n - 1)
                out = slots[:, slot, :]
                if use == "ot":
                    pe.wait_ge(o_done, H * t)
                    for j in range(J):
                        mm = nc.tensor.transpose(out[:, j * P:(j + 1) * P], o[:, 1 - u, j * P:(j + 1) * P],
                                                 ident[:, :])
                elif use == "wo":
                    pe.wait_ge(slot_free, n if is_tile(m, u, T) else n - NC)
                    mm = product3(nc, out[:, 0:D], lambda a, j: ot[:, a, j, :], lambda b, j: wo[b][:, j, :])
                elif use == "xt":
                    pe.wait_ge(xq_loaded, 16 * (t + 2))
                    for j in range(J):
                        mm = nc.tensor.transpose(out[:, j * P:(j + 1) * P], xq[:, j * P:(j + 1) * P],
                                                 ident[:, :])
                else:
                    if not (isinstance(n, int) and n < 2):
                        pe.wait_ge(slot_free, n - NC)
                    else:
                        pe.wait_ge(slot_free, 1)
                    for c in range(J):
                        mm = product3(nc, out[:, c * P:(c + 1) * P], lambda a, j: wq[a][:, j, c * P:(c + 1) * P],
                                      lambda b, j: xt[:, b, j, :])
                mm.then_inc(slot_full, 1)

            all_steps(pe, step, extra)

        @block.scalar
        def _(act):
            def step(m, u, h, place, _scores, exp, probs, tail):
                i = (2 * m + u) * H + h
                for c, (lo, width) in enumerate(CHUNKS):
                    if probs:
                        for g in (2 * c, 2 * c + 1):
                            act.wait_ge(turned, NG * (i - 2) + g + 1)
                            w = P * len(GROUPS[g])
                            nc.scalar.activation(pt[0][:, g, 0:w], ps_t[:, g % 2, 0:w], ACT.Copy, scale=P_S) \
                                .then_inc(pt_high, 1)
                    if tail and c == 1:
                        b = (h - 3) % 2
                        act.wait_ge(pv_done, i - 2)
                        act.wait_ge(rinv_ready, i - 2)
                        nc.scalar.activation(o_half[:, b, :], ps_pv[:, b, 0:KD], ACT.Copy,
                                             scale=rinv[:, b:b + 1]).then_inc(half_done, 1)
                    if exp:
                        b = (h - 1) % 2
                        if c == 0:
                            act.wait_ge(nmax_ready, i)
                        nc.scalar.activation(sp_sb[:, b, lo:lo + width], sp_sb[:, b, lo:lo + width], ACT.Exp,
                                             bias=nmax[:, b:b + 1], accum_out=esum[:, b, c:c + 1]) \
                            .then_inc(exp_done, 1)

            def extra(use, m, u, n, slot):
                if use == "wo":
                    return
                act.wait_ge(slot_full, n + 1)
                src = slots[:, slot, :]
                if use == "q" and not is_tile(m, u, -1):
                    act.wait_ge(q_spread, 64 * (2 * m + u + 1))
                dst, scale = part_of[use]
                nc.scalar.activation(dst[:, 0, :, :], src[:, 0:D].rearrange("p (j r) -> p j r", j=J),
                                     ACT.Copy, scale=scale).then_inc(slot_high, 1)

            all_steps(act, step, extra)

        @block.vector
        def _(dve):
            def step(m, u, h, place, scores, _exp, probs, tail):
                i = (2 * m + u) * H + h
                for c, (lo, width) in enumerate(CHUNKS):
                    if probs:
                        for g in (2 * c, 2 * c + 1):
                            dve.wait_ge(pt_high, NG * (i - 2) + g + 1)
                            w = P * len(GROUPS[g])
                            nc.vector.scalar_tensor_tensor(
                                out=pt[1][:, g, 0:w], in0=ps_t[:, g % 2, 0:w], scalar=P_S,
                                in1=pt[0][:, g, 0:w], op0=ALU.mult, op1=ALU.subtract).then_inc(pt_low, 1)
                        b = h % 2
                        if c == 0:
                            dve.wait_ge(exp_done, NC * (i - 1))
                            nc.vector.tensor_reduce(out=ssum[:, b:b + 1], in_=esum[:, b, :], axis=AX.X,
                                                    op=ALU.add).then_inc(ssum_ready, 1)
                        if c == 2:
                            dve.wait_ge(ssum_ready, i - 1)
                            nc.vector.reciprocal(rinv[:, b:b + 1], ssum[:, b:b + 1]).then_inc(rinv_ready, 1)
                    if scores:
                        n, slot = place[h, c], parity(m, u, (h, c))
                        if h == 0 and c == 0:
                            dve.wait_ge(bias_ready, 2 * m + u + 1)
                        wait_apart(dve, slot_full, n + 1, pad_clear)
                        nc.vector.tensor_tensor_reduce(
                            out=sp_sb[:, h % 2, lo:lo + width], in0=slots[:, slot, 0:width],
                            in1=adj[:, u, lo:lo + width], scale=1.0 / (Q_S * Q_S), scalar=-3.0e38,
                            op0=ALU.add, op1=ALU.max, accum_out=mx[:, h % 2, c:c + 1]).then_inc(slot_free, 1)
                    if tail and c == 1:
                        b, head = (h - 3) % 2, (h - 3) % H
                        ou = u if h >= 3 else 1 - u
                        dve.wait_ge(half_done, i - 2)
                        nc.vector.scalar_tensor_tensor(
                            out=o[:, ou, head * KD:(head + 1) * KD], in0=ps_pv[:, b, KD:2 * KD],
                            scalar=rinv[:, b:b + 1], in1=o_half[:, b, :], op0=ALU.mult, op1=ALU.add) \
                            .then_inc(o_done, 1)
                if scores:
                    dve.wait_ge(slot_free, place[h, NC - 1] + 1)
                    nc.vector.tensor_reduce(out=nmax[:, h % 2:h % 2 + 1], in_=mx[:, h % 2, :], axis=AX.X,
                                            op=ALU.max, negate=True).then_inc(nmax_ready, 1)
                    if h == 1 and not is_tile(m, u, T - 1):
                        diagonal(*after(m, u))
                    if h == 5 and not is_tile(m, u, 0):
                        norm.finish(nc, dve, *before(m, u))

            def diagonal(m, u):
                t = 2 * m + u
                dve.wait_ge(adj_loaded[u], 16 * m + 16)
                part = adj[:, u, bass.ds(t * P, P)]
                nc.vector.tensor_tensor(out=part, in0=part, in1=ident[:, :], op=ALU.max) \
                    .then_inc(diag_ready, 1)

            def highs(use, m, u):
                t = 2 * m + u
                if is_tile(m, u, -1):
                    return {"xt": 1, "q": 2}[use]
                if is_tile(m, u, T):
                    return 3 * T
                return 3 * t + {"ot": 2, "xt": 3, "q": 4}[use]

            def extra(use, m, u, n, slot):
                t = 2 * m + u
                src = slots[:, slot, :]
                if use == "wo":
                    um = 1 - u
                    m1, _ = before(m, u)
                    dve.wait_ge(slot_full, n + 1)
                    dve.wait_ge(xres_loaded[um], 16 * m1 + 16)
                    nc.vector.scalar_tensor_tensor(out=norm.r[:, :], in0=src[:, 0:D], scalar=1.0 / (O_S * W_S),
                                                   in1=xres[:, um, :], op0=ALU.mult, op1=ALU.add) \
                        .then_inc(slot_free, 1)
                    dve.wait_ge(slot_free, n + 1)
                    norm.statistics(nc, dve, t - 1)
                    return
                dve.wait_ge(slot_high, highs(use, m, u))
                dst, scale = part_of[use]
                nc.vector.scalar_tensor_tensor(
                    out=dst[:, 1, :, :], in0=src[:, 0:D].rearrange("p (j r) -> p j r", j=J), scalar=scale,
                    in1=dst[:, 0, :, :], op0=ALU.mult, op1=ALU.subtract).then_inc(slot_free, 1)

            dve.wait_ge(pad_clear, 1)
            diagonal(0, 0)
            all_steps(dve, step, extra)
            norm.finish(nc, dve, T // 2 - 1, 1)


def edge_attention(nc, x_rows, out_rows, adj_rows, ht, sup, natt, bias_row, degree, ident):
    with ExitStack() as ctx:
        s = Scope(nc, ctx, "edge")
        adj = s.sb("adj", [P, 2, N])
        bias = s.sb("bias", [P, N])
        junk = s.sb("junk", [P, N], F16)
        xres = s.sb("xres", [P, 2, D])
        sc = s.sb("scores", [P, 2, N])
        pt = [s.sb(f"pt_{a}", [P, 2, BANK], F16) for a in ("high", "low")]
        xb = s.sb("xb", [P, 2, D])
        mx, nmax = s.sb("mx", [P, NC]), s.sb("nmax", [P, 1])
        esum, ssum, rinv = s.sb("esum", [P, 2, NC]), s.sb("ssum", [P, 1]), s.sb("rinv", [P, 1])
        rscale = s.sb("rscale", [P, 2])
        norm = Norm(s)
        slots = s.ps("slots", [P, 2, CHUNK])
        ps_t = s.ps("ps_t", [P, 2, BANK])
        ps_o = s.ps("ps_o", [P, 2, BANK])

        adj_loaded = [s.sem(f"adj_loaded{u}") for u in range(2)]
        xres_loaded = [s.sem(f"xres_loaded{u}") for u in range(2)]
        bias_ready = s.sem("bias_ready")
        slot_full = s.sem("slot_full")
        slot_free = s.sem("slot_free")
        nmax_ready = s.sem("nmax_ready")
        exp_done = s.sem("exp_done")
        weighed = s.sem("weighed")
        degree_ready = s.sem("degree_ready")
        ssum_ready = s.sem("ssum_ready")
        rinv_ready = s.sem("rinv_ready")
        rscale_ready = s.sem("rscale_ready")
        turned = s.sem("turned")
        pt_high = s.sem("pt_high")
        pt_low = s.sem("pt_low")
        used = s.sem("used")
        xb_ready = s.sem("xb_ready")
        r_ready = s.sem("r_ready")
        block = ctx.enter_context(nc.Block())

        def tiles(eng, first, both, last):
            first(0, 0)
            both(0, 1)
            both(1, 0)
            pairs(eng, 3, T - 1, both)
            both(T // 2 - 1, 1)
            last(T // 2 - 1, 1)

        @block.sync
        def _(sp):
            def load(m, u):
                t = 2 * m + u
                if not (isinstance(m, int) and m == 0):
                    sp.wait_ge(weighed, NC * (t - 1))
                    sp.wait_ge(degree_ready, t - 1)
                    sp.wait_ge(xb_ready, t - 1)
                sp.dma_start(adj[:, u, :], adj_rows[bass.ds(t * P, P), :]).then_inc(adj_loaded[u], 16)
                sp.dma_start(xres[:, u, :], x_rows[bass.ds(t * P, P), :]).then_inc(xres_loaded[u], 16)

            def late(m, u):
                load(m, u)
                if not is_tile(m, u, 2):
                    norm.store(sp, out_rows, *before(*before(*before(m, u))))

            load(0, 0)
            load(0, 1)
            late(1, 0)
            pairs(sp, 3, T - 1, late)
            late(T // 2 - 1, 1)
            for t in range(T - 3, T):
                norm.store(sp, out_rows, t // 2, t % 2)
            norm.all_stored(sp)

        @block.gpsimd
        def _(pool):
            norm.exponent(nc, pool)

            def prepare(m, u):
                t = 2 * m + u
                if not is_tile(m, u, 0):
                    wait_apart(pool, slot_free, NC * t, norm.power_ready)
                wait_apart(pool, adj_loaded[u], 16 * m + 16, norm.power_ready)
                nc.gpsimd.tensor_scalar(out=bias[:, :], in0=adj[:, u, :], scalar1=0.0, scalar2=BIG2 * Q_S * Q_S,
                                        op0=ALU.is_le, op1=ALU.mult).then_inc(bias_ready, 1)
                if not (isinstance(m, int) and m == 0):
                    pool.wait_ge(r_ready, t - 1)
                pool.wait_ge(xres_loaded[u], 16 * m + 16)
                nc.gpsimd.tensor_tensor(out=xb[:, u, :], in0=xres[:, u, :], in1=bias_row[:, :], op=ALU.add) \
                    .then_inc(xb_ready, 1)

            def both(m, u):
                prepare(m, u)
                norm.deviation(nc, pool, 2 * m + u - 2)

            prepare(0, 0)
            prepare(0, 1)
            pairs(pool, 2, T, both)
            norm.deviation(nc, pool, T - 2)
            norm.deviation(nc, pool, T - 1)

        @block.tensor
        def _(pe):
            def scores(m, u, c):
                t, (lo, width) = 2 * m + u, CHUNKS[c]
                n, slot = NC * t + c, (NC * u + c) % 2
                if not (isinstance(n, int) and n < 2):
                    pe.wait_ge(slot_free, n - 1)
                banks = [(z, min(BANK, width - z)) for z in range(0, width, BANK)]
                terms = [(a, b, j) for j in range(J) for a, b in ((0, 0), (0, 1), (1, 0))]
                for k, (a, b, j) in enumerate(terms):
                    for z, w in banks:
                        mm = nc.tensor.matmul(slots[:, slot, z:z + w], ht[a][:, j, bass.ds(t * P, P)],
                                              ht[b][:, j, lo + z:lo + z + w],
                                              start=k == 0, stop=k == len(terms) - 1)
                mm.then_inc(slot_full, 1)

            def turn(m, u, g):
                t = 2 * m + u
                n = NG * t + g
                if g % 2 == 0:
                    pe.wait_ge(weighed, NC * t + g // 2 + 1)
                if not (isinstance(n, int) and n < 2):
                    pe.wait_ge(pt_low, n - 1)
                for k in GROUPS[g]:
                    r = rows_of(k)
                    mm = nc.tensor.transpose(ps_t[0:r, g % 2, (k % GB) * P:(k % GB + 1) * P],
                                             sc[:, u, k * P:k * P + r], ident[:, :])
                mm.then_inc(turned, 1)

            def multiply(m, u, g):
                t = 2 * m + u
                pe.wait_ge(pt_low, NG * t + g + 1)
                if g == 0 and not (isinstance(m, int) and m == 0):
                    pe.wait_ge(r_ready, t - 1)
                for k in GROUPS[g]:
                    r = rows_of(k)
                    for a, b in ((0, 0), (0, 1), (1, 0)):
                        mm = nc.tensor.matmul(
                            ps_o[:, u, :], pt[a][0:r, g % 2, (k % GB) * P:(k % GB + 1) * P],
                            sup[b][0:r, k, :], start=k == 0 and a + b == 0,
                            stop=k == T - 1 and a == 1)
                mm.then_inc(used, 1)

            def products(m, u):
                for g in range(NG):
                    multiply(m, u, g)
                    if g + 2 < NG:
                        turn(m, u, g + 2)

            def first(m, u):
                for c in range(NC):
                    scores(m, u, c)

            def both(m, u):
                for c in range(NC - 1):
                    scores(m, u, c)
                turn(*before(m, u), 0)
                turn(*before(m, u), 1)
                scores(m, u, NC - 1)
                products(*before(m, u))

            def last(m, u):
                turn(m, u, 0)
                turn(m, u, 1)
                products(m, u)

            tiles(pe, first, both, last)

        @block.scalar
        def _(act):
            def exp(m, u, c):
                t, (lo, width) = 2 * m + u, CHUNKS[c]
                if c == 0:
                    act.wait_ge(nmax_ready, t + 1)
                    if not (isinstance(m, int) and m == 0):
                        act.wait_ge(ssum_ready, t - 1)
                nc.scalar.activation(sc[:, u, lo:lo + width], sc[:, u, lo:lo + width], ACT.Exp,
                                     bias=nmax[:, :], accum_out=esum[:, u, c:c + 1]).then_inc(exp_done, 1)

            def high(m, u, g):
                n = NG * (2 * m + u) + g
                act.wait_ge(turned, n + 1)
                if not (isinstance(n, int) and n < 2):
                    act.wait_ge(used, n - 1)
                w = P * len(GROUPS[g])
                nc.scalar.activation(pt[0][:, g % 2, 0:w], ps_t[:, g % 2, 0:w], ACT.Copy, scale=P_S) \
                    .then_inc(pt_high, 1)

            def sum_degree(m, u):
                t = 2 * m + u
                act.wait_ge(adj_loaded[u], 16 * m + 16)
                if not is_tile(m, u, 0):
                    act.wait_ge(degree_ready, t)
                nc.scalar.activation(junk[:, :], adj[:, u, :], ACT.Copy, accum_out=degree[:, bass.ds(t, 1)]) \
                    .then_inc(degree_ready, 1)

            def first(m, u):
                for c in range(NC):
                    exp(m, u, c)

            def both(m, u):
                back = before(m, u)
                sum_degree(*back)
                high(*back, 0)
                for c in range(NC):
                    high(*back, 2 * c + 1)
                    exp(m, u, c)
                    if 2 * c + 2 < NG:
                        high(*back, 2 * c + 2)

            def last(m, u):
                sum_degree(m, u)
                for g in range(NG):
                    high(m, u, g)

            tiles(act, first, both, last)

        @block.vector
        def _(dve):
            def mask(m, u, c):
                t, (lo, width) = 2 * m + u, CHUNKS[c]
                if c == 0:
                    dve.wait_ge(bias_ready, t + 1)
                wait_apart(dve, slot_full, NC * t + c + 1, norm.power_ready)
                nc.vector.tensor_tensor_reduce(
                    out=sc[:, u, lo:lo + width], in0=slots[:, (NC * u + c) % 2, 0:width],
                    in1=bias[:, lo:lo + width], scale=1.0 / (Q_S * Q_S), scalar=-3.0e38,
                    op0=ALU.add, op1=ALU.max, accum_out=mx[:, c:c + 1]).then_inc(slot_free, 1)
                if c == NC - 1:
                    dve.wait_ge(slot_free, NC * (t + 1))
                    if not is_tile(m, u, 0):
                        dve.wait_ge(exp_done, NC * t)
                    nc.vector.tensor_reduce(out=nmax[:, :], in_=mx[:, :], axis=AX.X, op=ALU.max, negate=True) \
                        .then_inc(nmax_ready, 1)

            def weigh(m, u, c):
                t, (lo, width) = 2 * m + u, CHUNKS[c]
                dve.wait_ge(exp_done, NC * t + c + 1)
                nc.vector.tensor_tensor(out=sc[:, u, lo:lo + width], in0=sc[:, u, lo:lo + width],
                                        in1=adj[:, u, lo:lo + width], op=ALU.mult).then_inc(weighed, 1)

            def scale(m, u):
                t = 2 * m + u
                nc.vector.tensor_reduce(out=ssum[:, :], in_=esum[:, u, :], axis=AX.X, op=ALU.add) \
                    .then_inc(ssum_ready, 1)
                dve.wait_ge(ssum_ready, t + 1)
                nc.vector.reciprocal(rinv[:, :], ssum[:, :]).then_inc(rinv_ready, 1)
                dve.wait_ge(rinv_ready, t + 1)
                nc.vector.scalar_tensor_tensor(out=rscale[:, u:u + 1], in0=rinv[:, :], scalar=1.0 / (P_S * V_S),
                                               in1=natt[:, bass.ds(t, 1)], op0=ALU.mult, op1=ALU.mult) \
                    .then_inc(rscale_ready, 1)

            def low(m, u, g):
                dve.wait_ge(pt_high, NG * (2 * m + u) + g + 1)
                w = P * len(GROUPS[g])
                nc.vector.scalar_tensor_tensor(
                    out=pt[1][:, g % 2, 0:w], in0=ps_t[:, g % 2, 0:w], scalar=P_S,
                    in1=pt[0][:, g % 2, 0:w], op0=ALU.mult, op1=ALU.subtract).then_inc(pt_low, 1)

            def finish(m, u):
                t = 2 * m + u
                dve.wait_ge(used, NG * (t + 1))
                dve.wait_ge(rscale_ready, t + 1)
                dve.wait_ge(xb_ready, t + 1)
                nc.vector.scalar_tensor_tensor(out=norm.r[:, :], in0=ps_o[:, u, :], scalar=rscale[:, u:u + 1],
                                               in1=xb[:, u, :], op0=ALU.mult, op1=ALU.add).then_inc(r_ready, 1)
                dve.wait_ge(r_ready, t + 1)
                norm.statistics(nc, dve, t)
                norm.finish(nc, dve, m, u)

            def first(m, u):
                for c in range(NC):
                    mask(m, u, c)
                for c in range(NC):
                    weigh(m, u, c)
                scale(m, u)

            def both(m, u):
                back = before(m, u)
                for c in range(NC - 1):
                    mask(m, u, c)
                low(*back, 0)
                mask(m, u, NC - 1)
                for c in range(NC):
                    low(*back, 2 * c + 1)
                    if 2 * c + 2 < NG:
                        low(*back, 2 * c + 2)
                    weigh(m, u, c)
                scale(m, u)
                finish(*back)

            def last(m, u):
                for g in range(NG):
                    low(m, u, g)
                finish(m, u)

            tiles(dve, first, both, last)


def node_attention(nc, z, natt):
    with ExitStack() as ctx:
        s = Scope(nc, ctx, "node")
        m1, m2, nm = s.sb("m1", [P, 1]), s.sb("m2", [P, 1]), s.sb("nm", [P, 1])
        e, s1, s2, r = s.sb("e", [P, T]), s.sb("s1", [P, 1]), s.sb("s2", [P, 1]), s.sb("r", [P, 1])
        row_max, all_max = s.sem("row_max"), s.sem("all_max")
        neg_max, exps = s.sem("neg_max"), s.sem("exps")
        all_sum, recip, done = s.sem("all_sum"), s.sem("recip"), s.sem("done")
        block = ctx.enter_context(nc.Block())

        @block.gpsimd
        def _(pool):
            pool.wait_ge(row_max, 1)
            nc.gpsimd.partition_all_reduce(m2[:, :], m1[:, :], P, bass.bass_isa.ReduceOp.max) \
                .then_inc(all_max, 1)
            pool.wait_ge(exps, 1)
            nc.gpsimd.partition_all_reduce(s2[:, :], s1[:, :], P, bass.bass_isa.ReduceOp.add) \
                .then_inc(all_sum, 1)

        @block.scalar
        def _(act):
            act.wait_ge(all_max, 1)
            nc.scalar.mul(nm[:, :], m2[:, :], -1.0).then_inc(neg_max, 1)
            act.wait_ge(neg_max, 1)
            nc.scalar.activation(e[:, :], z[:, :], ACT.Exp, bias=nm[:, :], accum_out=s1[:, :]).then_inc(exps, 1)

        @block.vector
        def _(dve):
            nc.vector.tensor_reduce(out=m1[:, :], in_=z[:, :], axis=AX.X, op=ALU.max).then_inc(row_max, 1)
            dve.wait_ge(all_sum, 1)
            nc.vector.reciprocal(r[:, :], s2[:, :]).then_inc(recip, 1)
            dve.wait_ge(recip, 1)
            nc.vector.tensor_scalar(out=natt[:, :], in0=e[:, :], scalar1=r[:, :], scalar2=None, op0=ALU.mult) \
                .then_inc(done, 1)


def aggregate(nc, tag, x_rows, out_rows, adj_cols, y, bias_row, ident, dcol=None):
    with ExitStack() as ctx:
        s = Scope(nc, ctx, tag)
        a32 = s.sb("adj32", [P, 2, T, P])
        a16 = s.sb("adj16", [P, 2, T, P], F16)
        xres = s.sb("xres", [P, 2, D])
        act_in = s.sb("act_in", [P, D])
        norm = Norm(s)
        ps = s.ps("ps", [P, 2, BANK])
        adj_loaded = [s.sem(f"adj_loaded{u}") for u in range(2)]
        xres_loaded = [s.sem(f"xres_loaded{u}") for u in range(2)]
        narrowed = s.sem("narrowed")
        diag_ready = s.sem("diag_ready")
        summed = s.sem("summed")
        biased = s.sem("biased")
        r_ready = s.sem("r_ready")
        block = ctx.enter_context(nc.Block())

        @block.sync
        def _(sp):
            def load(m, u):
                t = 2 * m + u
                if not (isinstance(m, int) and m == 0):
                    sp.wait_ge(narrowed, t - 1)
                    sp.wait_ge(r_ready, t - 1)
                sp.dma_start(a32[:, u, :, :], adj_cols[bass.ds(t, 1), :, :, :].rearrange("o p k q -> (o p) k q")) \
                    .then_inc(adj_loaded[u], 16)
                sp.dma_start(xres[:, u, :], x_rows[bass.ds(t * P, P), :]).then_inc(xres_loaded[u], 16)

            def late(m, u):
                load(m, u)
                norm.store(sp, out_rows, *before(*before(m, u)))

            load(0, 0)
            load(0, 1)
            pairs(sp, 2, T, late)
            norm.store(sp, out_rows, T // 2 - 1, 0)
            norm.store(sp, out_rows, T // 2 - 1, 1)
            norm.all_stored(sp)

        @block.gpsimd
        def _(pool):
            norm.exponent(nc, pool)
            pairs(pool, 0, T, lambda m, u: norm.deviation(nc, pool, 2 * m + u))

        @block.scalar
        def _(act):
            def step(m, u):
                act.wait_ge(adj_loaded[u], 16 * m + 16)
                if not (isinstance(m, int) and m == 0):
                    act.wait_ge(summed, 2 * m + u - 1)
                nc.scalar.activation(a16[:, u, :, :], a32[:, u, :, :], ACT.Copy).then_inc(narrowed, 1)

            step(0, 0)
            step(0, 1)
            pairs(act, 2, T, step)

        @block.tensor
        def _(pe):
            def step(m, u):
                t = 2 * m + u
                pe.wait_ge(narrowed if dcol is None else diag_ready, t + 1)
                if not (isinstance(m, int) and m == 0):
                    pe.wait_ge(biased, t - 1)
                for k in range(T):
                    r = rows_of(k)
                    for b in range(2):
                        mm = nc.tensor.matmul(ps[:, u, :], a16[0:r, u, k, :], y[b][0:r, k, :],
                                              start=k == 0 and b == 0, stop=k == T - 1 and b == 1)
                mm.then_inc(summed, 1)

            step(0, 0)
            step(0, 1)
            pairs(pe, 2, T, step)

        @block.vector
        def _(dve):
            def identity(m, u):
                t = 2 * m + u
                dve.wait_ge(narrowed, t + 1)
                part = a16[:, u, bass.ds(t, 1), :].rearrange("p o q -> p (o q)")
                nc.vector.tensor_tensor(out=part, in0=part, in1=ident[:, :], op=ALU.add).then_inc(diag_ready, 1)

            def step(m, u):
                t = 2 * m + u
                dve.wait_ge(summed, t + 1)
                scale = 1.0 / V_S if dcol is None else dcol[:, bass.ds(t, 1)]
                nc.vector.scalar_tensor_tensor(out=act_in[:, :], in0=ps[:, u, :], scalar=scale,
                                               in1=bias_row[:, :], op0=ALU.mult, op1=ALU.add).then_inc(biased, 1)
                dve.wait_ge(biased, t + 1)
                dve.wait_ge(xres_loaded[u], 16 * m + 16)
                nc.vector.scalar_tensor_tensor(out=norm.r[:, :], in0=act_in[:, :], scalar=0.0,
                                               in1=xres[:, u, :], op0=ALU.max, op1=ALU.add).then_inc(r_ready, 1)
                dve.wait_ge(r_ready, t + 1)
                norm.statistics(nc, dve, t)
                norm.finish(nc, dve, m, u)

            if dcol is None:
                pairs(dve, 0, T, step)
            else:
                def both(m, u):
                    identity(*after(m, u))
                    step(m, u)

                identity(0, 0)
                pairs(dve, 0, T - 1, both)
                step(T // 2 - 1, 1)


def degree_scales(nc, degree, dy, dout):
    with ExitStack() as ctx:
        s = Scope(nc, ctx, "degree")
        d1, d, power = s.sb("d1", [P, T]), s.sb("d", [P, T]), s.sb("power", [P, T])
        d1_ready, d_ready = s.sem("d1_ready"), s.sem("d_ready")
        block = ctx.enter_context(nc.Block())

        @block.gpsimd
        def _(pool):
            nc.gpsimd.memset(power[:, :], -0.5).then_inc(d1_ready, 1)
            nc.gpsimd.tensor_scalar(out=d1[:, :], in0=degree[:, :], scalar1=1.0, scalar2=1.0, op0=ALU.mult,
                                    op1=ALU.add).then_inc(d1_ready, 1)
            pool.wait_ge(d1_ready, 2)
            nc.gpsimd.tensor_tensor(out=d[:, :], in0=d1[:, :], in1=power[:, :], op=ALU.pow).then_inc(d_ready, 1)

        @block.vector
        def _(dve):
            dve.wait_ge(d_ready, 1)
            nc.vector.tensor_scalar(out=dy[:, :], in0=d[:, :], scalar1=V_S * XW, scalar2=None, op0=ALU.mult)
            nc.vector.tensor_scalar(out=dout[:, :], in0=d[:, :], scalar1=1.0 / V_S, scalar2=None, op0=ALU.mult)


def build(nc, x, adj, adj_cols, wk, wq, wv, wo, w1, b1, w2, b2, node_w, edge_w, w3, b3, out, stop=99):
    x1, x2, x3 = (nc.dram_tensor(f"x{n}", [NP, D], F32).ap() for n in (1, 2, 3))
    with ExitStack() as outer:
        g = Scope(nc, outer, "all")
        ident = g.sb("ident", [P, P])
        rows = {name: g.sb(name, [P, D]) for name in ("b1_row", "b2_row", "b3_row", "node_row")}
        z, natt, degree = g.sb("z", [P, T]), g.sb("natt", [P, T]), g.sb("degree", [P, T])
        dy, dout = g.sb("dy", [P, T]), g.sb("dout", [P, T])
        cleared, made, loaded = g.sem("cleared"), g.sem("made"), g.sem("loaded")
        with nc.Block() as block:
            @block.gpsimd
            def _(pool):
                nc.gpsimd.memset(ident[:, :], 0.0).then_inc(cleared, 1)
                nc.gpsimd.memset(z[:, :], -3.0e38).then_inc(made, 1)
                pool.wait_ge(cleared, 1)
                nc.gpsimd.affine_select(out=ident[:, :], in_=ident[:, :], compare_op=ALU.not_equal, fill=1.0,
                                        base=0, pattern=[[-1, P]], channel_multiplier=1).then_inc(made, 1)

            @block.sync
            def _(sp):
                for name, src in (("b1_row", b1), ("b2_row", b2), ("b3_row", b3), ("node_row", node_w)):
                    sp.dma_start(rows[name][:, :], src.broadcast_to([P, D])).then_inc(loaded, 16)
                sp.wait_ge(loaded, 64)

        with ExitStack() as ctx:
            s = Scope(nc, ctx, "l0")
            kk = s.sb("kk", [P, H, NP], F16)
            vv = s.sb("vv", [P, T, H, P], F16)
            with ExitStack() as inner:
                w = Scope(nc, inner, "l0w")
                wkh, wkl, wvh, wvl = (w.sb(n, [P, J, D], F16) for n in ("wkh", "wkl", "wvh", "wvl"))
                weights_phase(nc, "w0", [(wk, wkh[:, :, :], wkl[:, :, :]), (wv, wvh[:, :, :], wvl[:, :, :])])

                def keys(t, bank):
                    part = bank.rearrange("p (c r) -> p c r", c=J)
                    return [(part[KD * e:KD * e + KD, :, :], kk[0:KD, e::2, bass.ds(t * P, P)],
                             kk[KD:P, e::2, bass.ds(t * P, P)], Q_S * XW) for e in range(2)]

                def values(t, bank):
                    part = bank.rearrange("p (h k) -> p h k", h=H)
                    dst = vv[:, bass.ds(t, 1), :, :].rearrange("p o h k -> p (o h) k")
                    return [(part, dst[:, :, 0:KD], dst[:, :, KD:P], V_S * XW)]

                project(nc, "p0", x, ident, [("cols", wkh, wkl, keys), ("rows", wvh, wvl, values)])
            wqs = [s.sb(f"wqs{a}", [P, J, D], F16) for a in range(2)]
            woh = [s.sb(f"wo{a}", [P, J, D], F16) for a in range(2)]
            weights_phase(nc, "w0o", [(wq, wqs[0][:, :, :], wqs[1][:, :, :]),
                                      (wo, woh[0][:, :, :], woh[1][:, :, :])])
            attention(nc, x, x1, adj, kk, vv, wqs, woh, ident)
        if stop == 0:
            return x1

        def split_rows(y):
            return lambda t, bank: [(bank, y[0][:, bass.ds(t, 1), :].rearrange("p o n -> p (o n)"),
                                     y[1][:, bass.ds(t, 1), :].rearrange("p o n -> p (o n)"), V_S * XW)]

        with ExitStack() as ctx:
            s = Scope(nc, ctx, "l1")
            y = [s.sb(f"y{a}", [P, T, D], F16) for a in range(2)]
            w = [s.sb(f"w{a}", [P, J, D], F16) for a in range(2)]
            weights_phase(nc, "w1", [(w1, w[0][:, :, :], w[1][:, :, :])])
            project(nc, "p1", x1, ident, [("rows", w[0], w[1], split_rows(y))])
            aggregate(nc, "a1", x1, x2, adj_cols, y, rows["b1_row"], ident)
        if stop == 1:
            return x2

        with ExitStack() as ctx:
            s = Scope(nc, ctx, "l2")
            ht = [s.sb(f"ht{a}", [P, J, NP], F16) for a in range(2)]
            sup = [s.sb(f"sup{a}", [P, T, D], F16) for a in range(2)]
            with ExitStack() as inner:
                w = Scope(nc, inner, "l2w")
                weh, wel, wsh, wsl = (w.sb(n, [P, J, D], F16) for n in ("weh", "wel", "wsh", "wsl"))
                weights_phase(nc, "w2", [(edge_w, weh[:, :, :], wel[:, :, :]), (w2, wsh[:, :, :], wsl[:, :, :])])

                def columns(t, bank):
                    return [(bank.rearrange("p (c r) -> p c r", c=J), ht[0][:, :, bass.ds(t * P, P)],
                             ht[1][:, :, bass.ds(t * P, P)], Q_S * XW)]

                project(nc, "p2", x2, ident, [("cols", weh, wel, columns), ("rows", wsh, wsl, split_rows(sup))],
                        score=(rows["node_row"], z))
            node_attention(nc, z, natt)
            edge_attention(nc, x2, x3, adj, ht, sup, natt, rows["b2_row"], degree, ident)
        if stop == 2:
            return x3

        with ExitStack() as ctx:
            s = Scope(nc, ctx, "l3")
            y = [s.sb(f"y{a}", [P, T, D], F16) for a in range(2)]
            w = [s.sb(f"w{a}", [P, J, D], F16) for a in range(2)]
            degree_scales(nc, degree, dy, dout)
            weights_phase(nc, "w3", [(w3, w[0][:, :, :], w[1][:, :, :])])
            project(nc, "p3", x3, ident, [("rows", w[0], w[1], split_rows(y))], row_scale=dy)
            aggregate(nc, "a3", x3, out, adj_cols, y, rows["b3_row"], ident, dcol=dout)


def kernel(x, adj, L0_gnn_Wks, L0_gnn_Wqs, L0_gnn_Wvs, L0_gnn_Wo, L1_gnn_W, L1_gnn_b, L2_gnn_weight,
           L2_gnn_bias, L2_gnn_node_w, L2_gnn_edge_w, L3_gnn_W, L3_gnn_b):
    import concourse.bacc as bacc
    from concourse.bass_utils import run_bass_kernel_spmd

    def heads(w):
        return np.asarray(w).transpose(1, 0, 2).reshape(D, D)

    def padded(a, shape):
        out = np.zeros(shape, np.float32)
        out[:a.shape[0], :a.shape[1]] = a
        return out

    x, adj = np.asarray(x), np.asarray(adj)
    cols = padded(adj.T, (NP, NP)).reshape(T, P, T, P).transpose(2, 1, 0, 3)
    arrays = {
        "x": padded(x, (NP, D)), "adj": padded(adj, (NP, N)), "adj_cols": cols,
        "wk": heads(L0_gnn_Wks), "wq": heads(L0_gnn_Wqs), "wv": heads(L0_gnn_Wvs),
        "wo": np.asarray(L0_gnn_Wo).reshape(H * KD, D),
        "w1": np.asarray(L1_gnn_W).T, "b1": np.asarray(L1_gnn_b).reshape(1, D),
        "w2": np.asarray(L2_gnn_weight), "b2": np.asarray(L2_gnn_bias).reshape(1, D),
        "node_w": np.asarray(L2_gnn_node_w).reshape(1, D), "edge_w": np.asarray(L2_gnn_edge_w),
        "w3": np.asarray(L3_gnn_W).T, "b3": np.asarray(L3_gnn_b).reshape(1, D),
    }
    arrays = {k: np.ascontiguousarray(v) for k, v in arrays.items()}
    nc = bacc.Bacc("TRN2", target_bir_lowering=False, num_devices=1)
    args = {k: nc.dram_tensor(f"in_{k}", v.shape, F32, kind="ExternalInput").ap() for k, v in arrays.items()}
    out = nc.dram_tensor("out_rows", (NP, D), F32, kind="ExternalOutput").ap()
    build(nc, **args, out=out)
    result = run_bass_kernel_spmd(nc, [{f"in_{k}": v for k, v in arrays.items()}], core_ids=[0])
    return result.results[0]["out_rows"][:N]
```

```python
from contextlib import ExitStack

import numpy as np

import concourse.bass as bass
from concourse import mybir

F32 = mybir.dt.float32
F16 = mybir.dt.float16
ALU = mybir.AluOpType
ACT = mybir.ActivationFunctionType
AX = mybir.AxisListType

P = 128
N = 2708
D = 512
H = 8
KD = 64
T = -(-N // P)
NP = T * P
LAST = N - (T - 1) * P
J = D // P
BANK = 512
CHUNK = 2 * BANK
CHUNKS = [(c, min(CHUNK, N - c)) for c in range(0, N, CHUNK)]
NC = len(CHUNKS)
GB = BANK // P
GROUPS = [list(range(g, min(g + GB, T))) for g in range(0, T, GB)]
NG = len(GROUPS)
CT = CHUNK // P
assert NC == 3 and T > 2 * CT + 1
assert NG == 2 * NC and T % 2 == 0 and N % P

X_S, W_S, Q_S, V_S, P_S, O_S = 16.0, 256.0, 16.0, 16.0, 1024.0, 16.0
XW = 1.0 / (X_S * W_S)
EPS = 1e-5
BIG0 = 1e16
BIG2 = -9000000000000000.0


def wait_apart(eng, sem, value, met):
    if not isinstance(value, int):
        value = eng.to_reg(value)
    eng.wait_ge(met, 1)
    eng.wait_ge(sem, value)


def rows_of(k):
    return P if k < T - 1 else LAST


class Scope:

    def __init__(self, nc, ctx, tag, layer=None):
        self.nc, self.ctx, self.tag = nc, ctx, tag
        self.sems = [] if layer is None else layer.sems
        if layer is None:
            ctx.callback(self.release)

    def release(self):
        if self.sems:
            self.nc.clear_and_free_semaphores(self.sems)
            self.nc.all_engine_barrier()

    def sb(self, name, shape, dt=F32):
        return self.ctx.enter_context(self.nc.sbuf_tensor(f"{self.tag}_{name}", shape, dt))

    def ps(self, name, shape):
        return self.ctx.enter_context(self.nc.psum_tensor(f"{self.tag}_{name}", shape, F32))

    def sem(self, name):
        self.sems.append(self.nc.alloc_semaphore(f"{self.tag}_{name}"))
        return self.sems[-1]


def product3(nc, out, lhs, rhs, first=True, last=True):
    terms = [(a, b, j) for j in range(J) for a, b in ((0, 0), (0, 1), (1, 0))]
    for n, (a, b, j) in enumerate(terms):
        mm = nc.tensor.matmul(out, lhs(a, j), rhs(b, j), start=first and n == 0,
                              stop=last and n == len(terms) - 1)
    return mm


class Weights:

    def __init__(self, s, name, specs):
        self.parts, self.loaded = [], []
        for n, (src, high, low) in enumerate(specs):
            stage = s.sb(f"{name}_stage{n}", [P, J, src.shape[1]])
            blocks = src.rearrange("(j p) n -> p j n", p=P)
            for half in range(2):
                js = slice(half * J // 2, (half + 1) * J // 2)
                self.parts.append((blocks[:, js, :], stage[:, js, :], high[:, js, :], low[:, js, :]))
                self.loaded.append(s.sem(f"{name}_loaded{n}{half}"))
        self.high_ready = s.sem(f"{name}_high")
        self.low_ready = s.sem(f"{name}_low")

    def load(self, sp):
        for (src, stage, _h, _l), loaded in zip(self.parts, self.loaded):
            sp.dma_start(stage, src).then_inc(loaded, 16)

    def split_high(self, nc, act):
        for (_s, stage, high, _l), loaded in zip(self.parts, self.loaded):
            act.wait_ge(loaded, 16)
            nc.scalar.activation(high, stage, ACT.Copy, scale=W_S).then_inc(self.high_ready, 1)

    def split_low(self, nc, dve):
        for n, (_s, stage, high, low) in enumerate(self.parts):
            dve.wait_ge(self.high_ready, n + 1)
            nc.vector.scalar_tensor_tensor(out=low, in0=stage, scalar=W_S, in1=high, op0=ALU.mult,
                                           op1=ALU.subtract).then_inc(self.low_ready, 1)

    def wait(self, pe, n):
        pe.wait_ge(self.low_ready, 2 * n + 2)


def pairs(eng, begin, end, step):
    turns = (end - begin) // 2
    with eng.Fori(0, turns) as i:
        for t in (begin, begin + 1):
            step(i + t // 2, t % 2)
    if (end - begin) % 2:
        step((end - 1) // 2, (end - 1) % 2)


def after(m, u):
    return (m, 1) if u == 0 else (m + 1, 0)


def project(nc, layer, tag, x_rows, ident, weights, jobs, score=None, degrees=None, xt_rows=None, later=(),
            prefetch=()):
    with ExitStack() as ctx:
        s = Scope(nc, ctx, tag, layer)
        x_in = s.sb("x_in", [P, 2, D])
        xt = s.sb("xt", [P, 2, 2, J, P], F16)
        junk = s.sb("junk", [P, D])
        ps_t = s.ps("ps_t", [P, 2, BANK])
        ps_job = [s.ps(f"ps_job{n}", [P, 2, BANK]) for n in range(len(jobs))]
        x_loaded = [s.sem(f"x_loaded{u}") for u in range(2)]
        turned = s.sem("turned")
        xt_high = s.sem("xt_high")
        xt_low = s.sem("xt_low")
        made = s.sem("made")
        out_high = s.sem("out_high")
        out_low = s.sem("out_low")
        weighed = s.sem("weighed")
        scored = s.sem("scored")
        xt_stored = [s.sem(f"xt_stored{u}") for u in range(2)]
        prefetched = s.sem("prefetched")
        nj = len(jobs)
        own, late_w = Weights(s, "w", weights), Weights(s, "later", later)
        row_scale = None
        if degrees is not None:
            degree, row_scale, dout = degrees
            d1, d, power = s.sb("d1", [P, T]), s.sb("d", [P, T]), s.sb("power", [P, T])
            d1_ready = s.sem("d1_ready")
            d_ready = s.sem("d_ready")
            dy_ready = s.sem("dy_ready")
        block = ctx.enter_context(nc.Block())

        if degrees is not None:
            @block.gpsimd
            def _(pool):
                nc.gpsimd.memset(power[:, :], -0.5).then_inc(d1_ready, 1)
                nc.gpsimd.tensor_scalar(out=d1[:, :], in0=degree[:, :], scalar1=1.0, scalar2=1.0, op0=ALU.mult,
                                        op1=ALU.add).then_inc(d1_ready, 1)
                pool.wait_ge(d1_ready, 2)
                nc.gpsimd.tensor_tensor(out=d[:, :], in0=d1[:, :], in1=power[:, :], op=ALU.pow) \
                    .then_inc(d_ready, 1)

        @block.sync
        def _(sp):
            def load(m, u):
                if not (isinstance(m, int) and m == 0):
                    sp.wait_ge(turned, 2 * m + u - 1)
                    if score is not None:
                        sp.wait_ge(scored, 2 * m + u - 1)
                sp.dma_start(x_in[:, u, :], x_rows[bass.ds((2 * m + u) * P, P), :]) \
                    .then_inc(x_loaded[u], 16)

            def keep(m, u):
                if xt_rows is not None:
                    sp.wait_ge(xt_low, 2 * m + u + 1)
                    sp.dma_start(xt_rows[bass.ds((2 * m + u) * P, P), :],
                                 xt[:, u, :, :, :].rearrange("p a j r -> p (a j r)")) \
                        .then_inc(xt_stored[u], 16)

            def late(m, u):
                load(m, u)
                keep(*before(*before(m, u)))

            load(0, 0)
            own.load(sp)
            load(0, 1)
            late_w.load(sp)
            late(1, 0)
            late(1, 1)
            for dst, src in prefetch:
                sp.dma_start(dst, src).then_inc(prefetched, 16)
            pairs(sp, 4, T, late)
            keep(T // 2 - 1, 0)
            keep(T // 2 - 1, 1)
            if prefetch:
                sp.wait_ge(prefetched, 16 * len(prefetch))
            if xt_rows is not None:
                for u in range(2):
                    sp.wait_ge(xt_stored[u], 16 * (T // 2))

        @block.tensor
        def _(pe):
            def turn(m, u):
                pe.wait_ge(x_loaded[u], 16 * m + 16)
                if not (isinstance(m, int) and m == 0):
                    pe.wait_ge(xt_low, 2 * m + u - 1)
                for j in range(J):
                    mm = nc.tensor.transpose(ps_t[:, u, j * P:(j + 1) * P],
                                             x_in[:, u, j * P:(j + 1) * P], ident[:, :])
                mm.then_inc(turned, 1)

            def multiply(m, u):
                pe.wait_ge(xt_low, 2 * m + u + 1)
                for n, (kind, wh, wl, _) in enumerate(jobs):
                    w = (wh, wl)
                    if is_tile(m, u, 0):
                        own.wait(pe, n)
                    if not (isinstance(m, int) and m == 0):
                        pe.wait_ge(out_low, nj * (2 * m + u - 2) + n + 1)
                    if kind == "rows":
                        mm = product3(nc, ps_job[n][:, u, :], lambda a, j: xt[:, u, a, j, :],
                                      lambda b, j: w[b][:, j, :])
                    else:
                        for c in range(J):
                            mm = product3(nc, ps_job[n][:, u, c * P:(c + 1) * P],
                                          lambda a, j: w[a][:, j, c * P:(c + 1) * P],
                                          lambda b, j: xt[:, u, b, j, :])
                    mm.then_inc(made, 1)

            def step(m, u):
                turn(*after(m, u))
                multiply(m, u)

            turn(0, 0)
            step(0, 0)
            step(0, 1)
            pairs(pe, 2, T - 1, step)
            multiply(T // 2 - 1, 1)

        @block.scalar
        def _(act):
            def split(m, u):
                act.wait_ge(turned, 2 * m + u + 1)
                if not (isinstance(m, int) and m == 0):
                    act.wait_ge(made, nj * (2 * m + u - 1))
                    if xt_rows is not None:
                        act.wait_ge(xt_stored[u], 16 * m)
                nc.scalar.activation(xt[:, u, 0, :, :], ps_t[:, u, :].rearrange("p (j r) -> p j r", j=J),
                                     ACT.Copy, scale=X_S).then_inc(xt_high, 1)

            def finish(m, u):
                t = 2 * m + u
                for n, (_, _, _, pieces) in enumerate(jobs):
                    act.wait_ge(made, nj * t + n + 1)
                    for part, high, _low, scale in pieces(t, ps_job[n][:, u, :]):
                        if row_scale is not None:
                            scale = row_scale[:, bass.ds(t, 1)]
                        op = nc.scalar.activation(high, part, ACT.Copy, scale=scale)
                    op.then_inc(out_high, 1)

            def step(m, u):
                split(*after(m, u))
                finish(m, u)

            split(0, 0)
            own.split_high(nc, act)
            if degrees is not None:
                act.wait_ge(dy_ready, 1)
            step(0, 0)
            pairs(act, 1, T - 1, step)
            late_w.split_high(nc, act)
            finish(T // 2 - 1, 1)

        @block.vector
        def _(dve):
            def split(m, u):
                t = 2 * m + u
                dve.wait_ge(xt_high, t + 1)
                nc.vector.scalar_tensor_tensor(
                    out=xt[:, u, 1, :, :], in0=ps_t[:, u, :].rearrange("p (j r) -> p j r", j=J), scalar=X_S,
                    in1=xt[:, u, 0, :, :], op0=ALU.mult, op1=ALU.subtract).then_inc(xt_low, 1)
                if score is not None:
                    node_w, z = score
                    r = LAST if isinstance(m, int) and t == T - 1 else P
                    dve.wait_ge(x_loaded[u], 16 * m + 16)
                    if not (isinstance(m, int) and t == 0):
                        dve.wait_ge(scored, t)
                    nc.vector.tensor_tensor(out=junk[0:r, :], in0=x_in[0:r, u, :], in1=node_w[0:r, :],
                                            op=ALU.mult).then_inc(weighed, 1)
                    dve.wait_ge(weighed, t + 1)
                    nc.vector.tensor_reduce(out=z[0:r, bass.ds(t, 1)], in_=junk[0:r, :], axis=AX.X,
                                            op=ALU.add).then_inc(scored, 1)

            def finish(m, u):
                t = 2 * m + u
                for n, (_, _, _, pieces) in enumerate(jobs):
                    dve.wait_ge(out_high, nj * t + n + 1)
                    for part, high, low, scale in pieces(t, ps_job[n][:, u, :]):
                        if row_scale is not None:
                            scale = row_scale[:, bass.ds(t, 1)]
                        op = nc.vector.scalar_tensor_tensor(out=low, in0=part, scalar=scale, in1=high,
                                                            op0=ALU.mult, op1=ALU.subtract)
                    op.then_inc(out_low, 1)

            def step(m, u):
                split(*after(m, u))
                finish(m, u)

            split(0, 0)
            own.split_low(nc, dve)
            if degrees is not None:
                dve.wait_ge(d_ready, 1)
                nc.vector.tensor_scalar(out=dout[:, :], in0=d[:, :], scalar1=1.0 / V_S, scalar2=None,
                                        op0=ALU.mult)
                nc.vector.tensor_scalar(out=row_scale[:, :], in0=d[:, :], scalar1=V_S * XW, scalar2=None,
                                        op0=ALU.mult).then_inc(dy_ready, 1)
                dve.wait_ge(dy_ready, 1)
            step(0, 0)
            pairs(dve, 1, T - 3, step)
            for t in range(T - 3, T - 1):
                step(t // 2, t % 2)
            late_w.split_low(nc, dve)
            finish(T // 2 - 1, 1)


def before(m, u):
    return (m, 0) if u == 1 else (m - 1, 1)


def is_tile(m, u, t):
    return isinstance(m, int) and 2 * m + u == t


class Norm:

    def __init__(self, s):
        self.r = s.sb("residual", [P, D])
        self.stats, self.mv = s.sb("stats", [P, 6]), s.sb("mv", [P, 2])
        self.veps, self.rstd = s.sb("veps", [P, 1]), s.sb("rstd", [P, 1])
        self.power = s.sb("power", [P, 1])
        self.out = s.sb("x_out", [P, 2, D])
        self.stats_ready = s.sem("stats_ready")
        self.mv_ready = s.sem("mv_ready")
        self.power_ready = s.sem("power_ready")
        self.veps_ready = s.sem("veps_ready")
        self.rstd_ready = s.sem("rstd_ready")
        self.x_ready = s.sem("x_ready")
        self.stored = [s.sem(f"x_stored{u}") for u in range(2)]

    def free(self, dve, m, u):
        if not is_tile(m, u, 0):
            dve.wait_ge(self.x_ready, 2 * m + u)

    def statistics(self, nc, dve, t):
        nc.vector.bn_stats(out=self.stats[:, :], in_=self.r[:, :]).then_inc(self.stats_ready, 1)
        wait_apart(dve, self.stats_ready, t + 1, self.power_ready)
        nc.vector.bn_aggr(out=self.mv[:, :], in_=self.stats[:, :]).then_inc(self.mv_ready, 1)

    def exponent(self, nc, pool):
        nc.gpsimd.memset(self.power[:, :], -0.5).then_inc(self.power_ready, 1)
        pool.wait_ge(self.power_ready, 1)

    def finish(self, nc, pool, m, u):
        t = 2 * m + u
        wait_apart(pool, self.mv_ready, t + 1, self.power_ready)
        nc.gpsimd.tensor_scalar(out=self.veps[:, :], in0=self.mv[:, 1:2], scalar1=1.0, scalar2=EPS,
                                op0=ALU.mult, op1=ALU.add).then_inc(self.veps_ready, 1)
        pool.wait_ge(self.veps_ready, t + 1)
        nc.gpsimd.tensor_tensor(out=self.rstd[:, :], in0=self.veps[:, :], in1=self.power[:, :],
                                op=ALU.pow).then_inc(self.rstd_ready, 1)
        if not (isinstance(m, int) and m == 0):
            wait_apart(pool, self.stored[u], 16 * m, self.power_ready)
        wait_apart(pool, self.rstd_ready, t + 1, self.power_ready)
        nc.gpsimd.tensor_scalar(out=self.out[:, u, :], in0=self.r[:, :], scalar1=self.mv[:, 0:1],
                                scalar2=self.rstd[:, :], op0=ALU.subtract, op1=ALU.mult) \
            .then_inc(self.x_ready, 1)

    def store(self, sp, rows, m, u):
        sp.wait_ge(self.x_ready, 2 * m + u + 1)
        sp.dma_start(rows[bass.ds((2 * m + u) * P, P), :], self.out[:, u, :]).then_inc(self.stored[u], 16)

    def all_stored(self, sp):
        for u in range(2):
            sp.wait_ge(self.stored[u], 16 * (T // 2))


def attention(nc, layer, x_rows, out_rows, xt_rows, adj_rows, kk, vv, wq, wo, ident):
    with ExitStack() as ctx:
        s = Scope(nc, ctx, "att", layer)
        adj = s.sb("adj", [P, 2, NP])
        xres = s.sb("xres", [P, 2, D])
        xt = s.sb("xt", [P, 2, J, P], F16)
        q_raw = s.sb("q_raw", [P, 2, J, P], F16)
        q = s.sb("q", [P, 2, 2, 2, J, P], F16)
        sp_sb = s.sb("scores", [P, 2, N])
        pt = [s.sb(f"pt_{a}", [P, NG, BANK], F16) for a in ("high", "low")]
        pv = s.sb("pv", [P, 2, H, P + 1])
        rinv = s.sb("rinv", [P, H, 1])
        o = s.sb("o", [P, 2, D])
        ot = s.sb("ot", [P, 2, J, P], F16)
        mx, nmax = s.sb("mx", [P, 2, NC]), s.sb("nmax", [P, 2])
        norm = Norm(s)
        slots = s.ps("slots", [P, 2, CHUNK])
        ps_t = s.ps("ps_t", [P, 2, BANK])
        ps_pv = s.ps("ps_pv", [P, BANK])
        ps_misc = s.ps("ps_misc", [P, BANK])

        adj_loaded = [s.sem(f"adj_loaded{u}") for u in range(2)]
        xres_loaded = [s.sem(f"xres_loaded{u}") for u in range(2)]
        xt_loaded = s.sem("xt_loaded")
        q_spread = s.sem("q_spread")
        pad_clear = s.sem("pad_clear")
        ones_ready = s.sem("ones_ready")
        diag_ready = s.sem("diag_ready")
        bias_ready = s.sem("bias_ready")
        slot_full = s.sem("slot_full")
        slot_free = s.sem("slot_free")
        misc_full = s.sem("misc_full")
        misc_high = s.sem("misc_high")
        misc_free = s.sem("misc_free")
        nmax_ready = s.sem("nmax_ready")
        exp_done = s.sem("exp_done")
        turned = s.sem("turned")
        pt_high = s.sem("pt_high")
        pt_low = s.sem("pt_low")
        pv_done = s.sem("pv_done")
        pv_out = s.sem("pv_out")
        pv_added = s.sem("pv_added")
        rinv_ready = s.sem("rinv_ready")
        o_done = s.sem("o_done")
        block = ctx.enter_context(nc.Block())

        EXTRA = {3: "ot", 4: "wo", 6: "q"}
        PER_TILE = NC * H
        assert PER_TILE % 2 == 0

        def extras(m, u):
            have = dict(EXTRA)
            if is_tile(m, u, 0):
                del have[3], have[4]
            if is_tile(m, u, T - 1):
                del have[6]
            return have

        def misc_of(use, m, u):
            t = 2 * m + u
            if is_tile(m, u, -1):
                return 0
            return 3 * t + {"ot": -1, "wo": 0, "q": 1}[use] - (1 if is_tile(m, u, T) else 0)

        def highs(use, m, u):
            return 1 if is_tile(m, u, -1) else 2 * (2 * m + u) + {"ot": 1, "q": 2}[use] \
                - (1 if is_tile(m, u, T) else 0)

        def all_steps(eng, step, extra):
            def tile(m, u):
                first = is_tile(m, u, 0)
                for h in range(H):
                    step(m, u, h, True, not first or h >= 1, not first or h >= 2, not first or h >= 3)
                    if h in extras(m, u):
                        extra(extras(m, u)[h], m, u)

            extra("q", -1, 1)
            tile(0, 0)
            pairs(eng, 1, T - 1, tile)
            tile(T // 2 - 1, 1)
            for h, flags in enumerate([(False, True, True, True), (False, False, True, True),
                                       (False, False, False, True)]):
                step(T // 2, 0, h, *flags)
            extra("ot", T // 2, 0)
            extra("wo", T // 2, 0)

        @block.sync
        def _(sp):
            def load_xt(t):
                sp.dma_start(xt[:, :, :, :].rearrange("p a j r -> p (a j r)"), xt_rows[bass.ds(t * P, P), :]) \
                    .then_inc(xt_loaded, 16)

            def spread(m, u):
                sp.wait_ge(misc_free, misc_of("q", m, u) + 1)
                for e in range(2):
                    for half in range(2):
                        sp.dma_start(q[half * KD:half * KD + KD, 1 - u, e, :, :, :],
                                     q_raw[e * KD:e * KD + KD, :, :, :]).then_inc(q_spread, 16)

            load_xt(0)
            sp.dma_start(adj[:, 0, 0:N], adj_rows[0:P, :]).then_inc(adj_loaded[0], 16)
            spread(-1, 1)

            def tile(m, u):
                t = 2 * m + u
                last = is_tile(m, u, T - 1)
                if not is_tile(m, u, 0):
                    sp.wait_ge(slot_free, PER_TILE * t)
                if not last:
                    m1, u1 = after(m, u)
                    sp.dma_start(adj[:, u1, 0:N], adj_rows[bass.ds((t + 1) * P, P), :]) \
                        .then_inc(adj_loaded[u1], 16)
                    sp.wait_ge(misc_full, misc_of("q", *before(m, u)) + 1)
                    load_xt(t + 1)
                if not (isinstance(m, int) and m == 0):
                    sp.wait_ge(norm.mv_ready, t - 1)
                sp.dma_start(xres[:, u, :], x_rows[bass.ds(t * P, P), :]).then_inc(xres_loaded[u], 16)
                if not last:
                    spread(m, u)
                if not is_tile(m, u, 0):
                    norm.store(sp, out_rows, *(before(m, u)))

            tile(0, 0)
            tile(0, 1)
            pairs(sp, 2, T - 1, tile)
            tile(T // 2 - 1, 1)
            norm.store(sp, out_rows, T // 2 - 1, 1)
            norm.all_stored(sp)

        @block.gpsimd
        def _(pool):
            nc.gpsimd.memset(adj[:, :, N:NP], 0.0).then_inc(pad_clear, 1)
            nc.gpsimd.memset(vv[:, :, :, P:P + 1], 1.0).then_inc(ones_ready, 1)
            norm.exponent(nc, pool)

            def bias(m, u):
                wait_apart(pool, diag_ready, 2 * m + u + 1, pad_clear)
                big = BIG0 * Q_S * Q_S
                nc.gpsimd.tensor_scalar(out=adj[:, u, 0:N], in0=adj[:, u, 0:N], scalar1=big, scalar2=-big,
                                        op0=ALU.mult, op1=ALU.add).then_inc(bias_ready, 1)

            def step(m, u, h, scores, _exp, _probs, tail):
                if tail and h == 2:
                    t, ou = 2 * m + u, 1 - u
                    by_head = o[:, ou, :].rearrange("p (h k) -> p h k", h=H)
                    pool.wait_ge(pv_out, H * t)
                    nc.gpsimd.tensor_tensor(out=by_head, in0=pv[:, ou, :, 0:KD], in1=pv[:, ou, :, KD:P],
                                            op=ALU.add).then_inc(pv_added, 1)
                    pool.wait_ge(pv_added, t)
                    pool.wait_ge(rinv_ready, t)
                    nc.gpsimd.tensor_tensor(out=by_head, in0=by_head,
                                            in1=rinv[:, :, :].broadcast_to([P, H, KD]), op=ALU.mult) \
                        .then_inc(o_done, 1)
                if scores and h == 1 and not is_tile(m, u, T - 1):
                    bias(*after(m, u))

            def extra(use, m, u):
                if use == "wo":
                    norm.finish(nc, pool, *before(m, u))

            bias(0, 0)
            all_steps(pool, step, extra)

        @block.tensor
        def _(pe):
            def values(i, h, g):
                pe.wait_ge(pt_low, NG * i + g + 1)
                for k in GROUPS[g]:
                    r = rows_of(k)
                    for a in (0, 1) if k < T - 1 else (1, 0):
                        cols = slice(a * KD, P + 1)
                        mm = nc.tensor.matmul(ps_pv[:, cols],
                                              pt[a][0:r, g, (k % GB) * P:(k % GB + 1) * P],
                                              vv[0:r, k, h, cols], start=k == 0 and a == 0,
                                              stop=k == T - 1 and a == 0)
                return mm

            def step(m, u, h, scores, _exp, probs, tail):
                t = 2 * m + u
                i = t * H + h
                for c, (lo, width) in enumerate(CHUNKS):
                    if probs:
                        pe.wait_ge(exp_done, NC * (i - 2) + c + 1)
                        for g in (2 * c, 2 * c + 1):
                            n = NG * (i - 2) + g
                            if not (isinstance(n, int) and n < 2):
                                pe.wait_ge(pt_low, n - 1)
                            for k in GROUPS[g]:
                                r = rows_of(k)
                                mm = nc.tensor.transpose(ps_t[0:r, g % 2, (k % GB) * P:(k % GB + 1) * P],
                                                         sp_sb[:, h % 2, k * P:k * P + r], ident[:, :])
                            mm.then_inc(turned, 1)
                    if scores:
                        n, slot = PER_TILE * t + NC * h + c, (NC * h + c) % 2
                        if c == 0 and h == 0:
                            pe.wait_ge(q_spread, 64 * (t + 1))
                        if not (isinstance(n, int) and n < 2):
                            pe.wait_ge(slot_free, n - 1)
                        for a in range(2):
                            for z in range(0, width, BANK):
                                w = min(BANK, width - z)
                                mm = nc.tensor.matmul(slots[:, slot, z:z + w], q[:, u, h % 2, a, h // 2, :],
                                                      kk[:, h, lo + z:lo + z + w],
                                                      start=a == 0, stop=a == 1)
                        mm.then_inc(slot_full, 1)
                    if c == 0:
                        if tail:
                            values(i - 3, (h - 3) % H, NG - 2)
                            values(i - 3, (h - 3) % H, NG - 1).then_inc(pv_done, 1)
                    elif probs:
                        if c == 1 and tail:
                            pe.wait_ge(pv_out, i - 2)
                        values(i - 2, (h - 2) % H, 2 * c - 2)
                        values(i - 2, (h - 2) % H, 2 * c - 1)

            def extra(use, m, u):
                t, n = 2 * m + u, misc_of(use, m, u)
                if not (isinstance(n, int) and n == 0):
                    pe.wait_ge(misc_free, n)
                if use == "ot":
                    pe.wait_ge(o_done, t)
                    for j in range(J):
                        mm = nc.tensor.transpose(ps_misc[:, j * P:(j + 1) * P], o[:, 1 - u, j * P:(j + 1) * P],
                                                 ident[:, :])
                elif use == "wo":
                    mm = product3(nc, ps_misc[:, 0:D], lambda a, j: ot[:, a, j, :], lambda b, j: wo[b][:, j, :])
                else:
                    pe.wait_ge(xt_loaded, 16 * (t + 2))
                    for c in range(J):
                        mm = product3(nc, ps_misc[:, c * P:(c + 1) * P],
                                      lambda a, j: wq[a][:, j, c * P:(c + 1) * P],
                                      lambda b, j: xt[:, b, j, :])
                mm.then_inc(misc_full, 1)

            pe.wait_ge(ones_ready, 1)
            all_steps(pe, step, extra)

        part_of = {"ot": (ot, O_S / V_S), "q": (q_raw, Q_S / 8.0 * XW)}

        @block.scalar
        def _(act):
            def step(m, u, h, _scores, exp, probs, tail):
                i = (2 * m + u) * H + h
                for c, (lo, width) in enumerate(CHUNKS):
                    if tail and c == 1:
                        head, ou = (h - 3) % H, u if h >= 3 else 1 - u
                        act.wait_ge(pv_done, i - 2)
                        if head == 0 and not (isinstance(m, int) and m == 0):
                            act.wait_ge(o_done, 2 * m + u - 1)
                        nc.scalar.activation(pv[:, ou, head, :], ps_pv[:, 0:P + 1], ACT.Copy) \
                            .then_inc(pv_out, 1)
                    if probs:
                        for g in (2 * c, 2 * c + 1):
                            act.wait_ge(turned, NG * (i - 2) + g + 1)
                            w = P * len(GROUPS[g])
                            nc.scalar.activation(pt[0][:, g, 0:w], ps_t[:, g % 2, 0:w], ACT.Copy, scale=P_S) \
                                .then_inc(pt_high, 1)
                    if exp:
                        b = (h - 1) % 2
                        if c == 0:
                            act.wait_ge(nmax_ready, i)
                        nc.scalar.activation(sp_sb[:, b, lo:lo + width], sp_sb[:, b, lo:lo + width], ACT.Exp,
                                             bias=nmax[:, b:b + 1]).then_inc(exp_done, 1)

            def extra(use, m, u):
                if use == "wo":
                    return
                act.wait_ge(misc_full, misc_of(use, m, u) + 1)
                if use == "q" and not is_tile(m, u, -1):
                    act.wait_ge(q_spread, 64 * (2 * m + u + 1))
                dst, scale = part_of[use]
                nc.scalar.activation(dst[:, 0, :, :], ps_misc[:, :].rearrange("p (j r) -> p j r", j=J),
                                     ACT.Copy, scale=scale).then_inc(misc_high, 1)

            all_steps(act, step, extra)

        @block.vector
        def _(dve):
            def step(m, u, h, scores, _exp, probs, tail):
                t = 2 * m + u
                i = t * H + h
                for c, (lo, width) in enumerate(CHUNKS):
                    if probs:
                        for g in (2 * c, 2 * c + 1):
                            dve.wait_ge(pt_high, NG * (i - 2) + g + 1)
                            w = P * len(GROUPS[g])
                            nc.vector.scalar_tensor_tensor(
                                out=pt[1][:, g, 0:w], in0=ps_t[:, g % 2, 0:w], scalar=P_S,
                                in1=pt[0][:, g, 0:w], op0=ALU.mult, op1=ALU.subtract).then_inc(pt_low, 1)
                    if scores:
                        if h == 0 and c == 0:
                            dve.wait_ge(bias_ready, t + 1)
                        wait_apart(dve, slot_full, PER_TILE * t + NC * h + c + 1, pad_clear)
                        nc.vector.tensor_tensor_reduce(
                            out=sp_sb[:, h % 2, lo:lo + width], in0=slots[:, (NC * h + c) % 2, 0:width],
                            in1=adj[:, u, lo:lo + width], scale=1.0 / (Q_S * Q_S), scalar=-3.0e38,
                            op0=ALU.add, op1=ALU.max, accum_out=mx[:, h % 2, c:c + 1]).then_inc(slot_free, 1)
                if scores:
                    dve.wait_ge(slot_free, PER_TILE * t + NC * (h + 1))
                    nc.vector.tensor_reduce(out=nmax[:, h % 2:h % 2 + 1], in_=mx[:, h % 2, :], axis=AX.X,
                                            op=ALU.max, negate=True).then_inc(nmax_ready, 1)
                    if h == 1 and not is_tile(m, u, T - 1):
                        diagonal(*after(m, u))
                if tail and h == 2:
                    dve.wait_ge(pv_out, H * t)
                    nc.vector.reciprocal(rinv[:, :, :], pv[:, 1 - u, :, P:P + 1]).then_inc(rinv_ready, 1)

            def diagonal(m, u):
                t = 2 * m + u
                dve.wait_ge(adj_loaded[u], 16 * m + 16)
                part = adj[:, u, bass.ds(t * P, P)]
                nc.vector.tensor_tensor(out=part, in0=part, in1=ident[:, :], op=ALU.max) \
                    .then_inc(diag_ready, 1)

            def extra(use, m, u):
                if use == "wo":
                    m1, u1 = before(m, u)
                    dve.wait_ge(misc_full, misc_of(use, m, u) + 1)
                    dve.wait_ge(xres_loaded[u1], 16 * m1 + 16)
                    norm.free(dve, m1, u1)
                    nc.vector.scalar_tensor_tensor(out=norm.r[:, :], in0=ps_misc[:, :], scalar=1.0 / (O_S * W_S),
                                                   in1=xres[:, u1, :], op0=ALU.mult, op1=ALU.add) \
                        .then_inc(misc_free, 1)
                    dve.wait_ge(misc_free, misc_of(use, m, u) + 1)
                    norm.statistics(nc, dve, 2 * m + u - 1)
                    return
                dve.wait_ge(misc_high, highs(use, m, u))
                dst, scale = part_of[use]
                nc.vector.scalar_tensor_tensor(
                    out=dst[:, 1, :, :], in0=ps_misc[:, :].rearrange("p (j r) -> p j r", j=J), scalar=scale,
                    in1=dst[:, 0, :, :], op0=ALU.mult, op1=ALU.subtract).then_inc(misc_free, 1)

            dve.wait_ge(pad_clear, 1)
            diagonal(0, 0)
            all_steps(dve, step, extra)


def edge_attention(nc, layer, x_rows, out_rows, scores_rows, adj_rows, adj, ht, sup, z, bias_row, degree, ident):
    with ExitStack() as ctx:
        s = Scope(nc, ctx, "edge", layer)
        bias = s.sb("bias", [P, N])
        junk = s.sb("junk", [P, N], F16)
        xres = s.sb("xres", [P, 2, D])
        sc = s.sb("scores", [P, 2, N])
        pt = [s.sb(f"pt_{a}", [P, 2, BANK], F16) for a in ("high", "low")]
        xb = s.sb("xb", [P, 2, D])
        raw = s.sb("raw", [P, N - CHUNK])
        mirror = s.sb("mirror", [P, 2, 2 * CT, P])
        mx, nmax = s.sb("mx", [P, NC]), s.sb("nmax", [P, 1])
        esum, ssum, rinv = s.sb("esum", [P, 2, NC]), s.sb("ssum", [P, 1]), s.sb("rinv", [P, 1])
        rscale = s.sb("rscale", [P, 2])
        z_max, z_all_max, z_neg_max = (s.sb(n, [P, 1]) for n in ("z_max", "z_all_max", "z_neg_max"))
        z_sum, z_all_sum, z_rinv = (s.sb(n, [P, 1]) for n in ("z_sum", "z_all_sum", "z_rinv"))
        z_exp, natt = s.sb("z_exp", [P, T]), s.sb("natt", [P, T])
        norm = Norm(s)
        slots = s.ps("slots", [P, 2, CHUNK])
        ps_t = s.ps("ps_t", [P, 2, BANK])
        ps_o = s.ps("ps_o", [P, 2, BANK])

        adj_loaded = [s.sem(f"adj_loaded{u}") for u in range(2)]
        xres_loaded = [s.sem(f"xres_loaded{u}") for u in range(2)]
        bias_ready = s.sem("bias_ready")
        slot_full = s.sem("slot_full")
        slot_free = s.sem("slot_free")
        nmax_ready = s.sem("nmax_ready")
        exp_done = s.sem("exp_done")
        weighed = s.sem("weighed")
        degree_ready = s.sem("degree_ready")
        ssum_ready = s.sem("ssum_ready")
        rinv_ready = s.sem("rinv_ready")
        rscale_ready = s.sem("rscale_ready")
        turned = s.sem("turned")
        pt_high = s.sem("pt_high")
        pt_low = s.sem("pt_low")
        used = s.sem("used")
        xb_ready = s.sem("xb_ready")
        r_ready = s.sem("r_ready")
        raw_copied = s.sem("raw_copied")
        raw_stored = s.sem("raw_stored")
        mirrored = [s.sem(f"mirrored{u}") for u in range(2)]
        z_max_ready = s.sem("z_max_ready")
        z_all_max_ready = s.sem("z_all_max_ready")
        z_neg_max_ready = s.sem("z_neg_max_ready")
        z_exp_ready = s.sem("z_exp_ready")
        z_all_sum_ready = s.sem("z_all_sum_ready")
        z_rinv_ready = s.sem("z_rinv_ready")
        natt_ready = s.sem("natt_ready")
        block = ctx.enter_context(nc.Block())

        def tiles(eng, first, both, last):
            first(0, 0)
            both(0, 1, 0)
            both(1, 0, 0)
            for band in range(NC):
                pairs(eng, max(3, band * CT), min((band + 1) * CT, T - 1), lambda m, u: both(m, u, band))
            both(T // 2 - 1, 1, NC - 1)
            last(T // 2 - 1, 1)

        def copies(t, band):
            return (2 * t, CT + t, 3 * CT)[band]

        @block.sync
        def _(sp):
            def load(m, u):
                t = 2 * m + u
                if not (isinstance(m, int) and m == 0):
                    sp.wait_ge(weighed, NC * (t - 1))
                    sp.wait_ge(degree_ready, t - 1)
                    sp.dma_start(adj[:, u, :], adj_rows[bass.ds(t * P, P), :]).then_inc(adj_loaded[u], 16)
                    sp.wait_ge(xb_ready, t - 1)
                sp.dma_start(xres[:, u, :], x_rows[bass.ds(t * P, P), :]).then_inc(xres_loaded[u], 16)

            def store_raw(m, u, band):
                if band < NC - 1:
                    t = 2 * m + u
                    sp.wait_ge(raw_copied, copies(t, band) + NC - 1 - band)
                    sp.dma_start(scores_rows[bass.ds(t * P, P), (band + 1) * CHUNK:N],
                                 raw[:, band * CHUNK:]).then_inc(raw_stored, 16)

            def load_mirror(m, u, band):
                if band > 0:
                    t, k = 2 * m + u, band * CT
                    w = LAST if is_tile(m, u, T - 1) else P
                    sp.wait_ge(raw_stored, 16 * k)
                    sp.wait_ge(slot_full, NC * (t - 1))
                    sp.dma_start(mirror[:, u, 0:k, 0:w],
                                 scores_rows[0:k * P, bass.ds(t * P, w)].rearrange("(k p) q -> p k q", p=P)) \
                        .then_inc(mirrored[u], 16)

            def late(m, u, last_band, band):
                load(m, u)
                store_raw(*before(m, u), last_band)
                load_mirror(m, u, band)
                if not is_tile(m, u, 2):
                    norm.store(sp, out_rows, *before(*before(*before(m, u))))

            load(0, 0)
            load(0, 1)
            store_raw(0, 0, 0)
            late(1, 0, 0, 0)
            pairs(sp, 3, CT, lambda m, u: late(m, u, 0, 0))
            for band in range(1, NC):
                late(band * CT // 2, 0, band - 1, band)
                pairs(sp, band * CT + 1, min((band + 1) * CT, T - 1), lambda m, u: late(m, u, band, band))
            late(T // 2 - 1, 1, NC - 1, NC - 1)
            for t in range(T - 3, T):
                norm.store(sp, out_rows, t // 2, t % 2)
            norm.all_stored(sp)

        @block.gpsimd
        def _(pool):
            norm.exponent(nc, pool)

            def prepare(m, u):
                t = 2 * m + u
                if not is_tile(m, u, 0):
                    wait_apart(pool, slot_free, NC * t, norm.power_ready)
                if not (isinstance(m, int) and m == 0):
                    wait_apart(pool, adj_loaded[u], 16 * m, norm.power_ready)
                nc.gpsimd.tensor_scalar(out=bias[:, :], in0=adj[:, u, :], scalar1=0.0, scalar2=BIG2 * Q_S * Q_S,
                                        op0=ALU.is_le, op1=ALU.mult).then_inc(bias_ready, 1)
                if not (isinstance(m, int) and m == 0):
                    pool.wait_ge(r_ready, t - 1)
                pool.wait_ge(xres_loaded[u], 16 * m + 16)
                nc.gpsimd.tensor_tensor(out=xb[:, u, :], in0=xres[:, u, :], in1=bias_row[:, :], op=ALU.add) \
                    .then_inc(xb_ready, 1)

            def both(m, u):
                prepare(m, u)
                norm.finish(nc, pool, *before(*before(m, u)))

            prepare(0, 0)
            pool.wait_ge(z_max_ready, 1)
            nc.gpsimd.partition_all_reduce(z_all_max[:, :], z_max[:, :], P, bass.bass_isa.ReduceOp.max) \
                .then_inc(z_all_max_ready, 1)
            prepare(0, 1)
            pool.wait_ge(z_exp_ready, 1)
            nc.gpsimd.partition_all_reduce(z_all_sum[:, :], z_sum[:, :], P, bass.bass_isa.ReduceOp.add) \
                .then_inc(z_all_sum_ready, 1)
            both(1, 0)
            both(1, 1)
            pairs(pool, 4, T, both)
            norm.finish(nc, pool, T // 2 - 1, 0)
            norm.finish(nc, pool, T // 2 - 1, 1)

        @block.tensor
        def _(pe):
            def scores(m, u, c, band):
                t, (lo, width) = 2 * m + u, CHUNKS[c]
                n, slot = NC * t + c, (NC * u + c) % 2
                if not (isinstance(n, int) and n < 2):
                    pe.wait_ge(slot_free, n - 1)
                if c == 0 and band < 2 and not is_tile(m, u, 0):
                    pe.wait_ge(raw_copied, 2 * t - 1 if band == 0 else 2 * CT - 1)
                if c == 1 and not is_tile(m, u, 0):
                    pe.wait_ge(raw_copied, copies(t, band))
                if c < band:
                    if c == 0:
                        pe.wait_ge(mirrored[u], 16 * (m - CT // 2 + 1))
                    for k in range(CT):
                        mm = nc.tensor.transpose(slots[:, slot, k * P:(k + 1) * P],
                                                 mirror[:, u, c * CT + k, :], ident[:, :])
                    mm.then_inc(slot_full, 1)
                    return
                banks = [(z, min(BANK, width - z)) for z in range(0, width, BANK)]
                terms = [(a, b, j) for j in range(J) for a, b in ((0, 0), (0, 1), (1, 0))]
                for k, (a, b, j) in enumerate(terms):
                    for z, w in banks:
                        mm = nc.tensor.matmul(slots[:, slot, z:z + w], ht[a][:, j, bass.ds(t * P, P)],
                                              ht[b][:, j, lo + z:lo + z + w],
                                              start=k == 0, stop=k == len(terms) - 1)
                mm.then_inc(slot_full, 1)

            def turn(m, u, g):
                t = 2 * m + u
                n = NG * t + g
                if g % 2 == 0:
                    pe.wait_ge(weighed, NC * t + g // 2 + 1)
                if not (isinstance(n, int) and n < 2):
                    pe.wait_ge(pt_low, n - 1)
                for k in GROUPS[g]:
                    r = rows_of(k)
                    mm = nc.tensor.transpose(ps_t[0:r, g % 2, (k % GB) * P:(k % GB + 1) * P],
                                             sc[:, u, k * P:k * P + r], ident[:, :])
                mm.then_inc(turned, 1)

            def multiply(m, u, g):
                t = 2 * m + u
                pe.wait_ge(pt_low, NG * t + g + 1)
                if g == 0 and not (isinstance(m, int) and m == 0):
                    pe.wait_ge(r_ready, t - 1)
                for k in GROUPS[g]:
                    r = rows_of(k)
                    for a, b in ((0, 0), (0, 1), (1, 0)):
                        mm = nc.tensor.matmul(
                            ps_o[:, u, :], pt[a][0:r, g % 2, (k % GB) * P:(k % GB + 1) * P],
                            sup[b][0:r, k, :], start=k == 0 and a + b == 0,
                            stop=k == T - 1 and a == 1)
                mm.then_inc(used, 1)

            def products(m, u):
                for g in range(NG):
                    multiply(m, u, g)
                    if g + 2 < NG:
                        turn(m, u, g + 2)

            def first(m, u):
                for c in range(NC):
                    scores(m, u, c, 0)

            def both(m, u, band):
                for c in range(NC - 1):
                    scores(m, u, c, band)
                turn(*before(m, u), 0)
                turn(*before(m, u), 1)
                scores(m, u, NC - 1, band)
                products(*before(m, u))

            def last(m, u):
                turn(m, u, 0)
                turn(m, u, 1)
                products(m, u)

            tiles(pe, first, both, last)

        @block.scalar
        def _(act):
            def exp(m, u, c):
                t, (lo, width) = 2 * m + u, CHUNKS[c]
                if c == 0:
                    act.wait_ge(nmax_ready, t + 1)
                    if not (isinstance(m, int) and m == 0):
                        act.wait_ge(ssum_ready, t - 1)
                nc.scalar.activation(sc[:, u, lo:lo + width], sc[:, u, lo:lo + width], ACT.Exp,
                                     bias=nmax[:, :], accum_out=esum[:, u, c:c + 1]).then_inc(exp_done, 1)

            def high(m, u, g):
                n = NG * (2 * m + u) + g
                act.wait_ge(turned, n + 1)
                if not (isinstance(n, int) and n < 2):
                    act.wait_ge(used, n - 1)
                w = P * len(GROUPS[g])
                nc.scalar.activation(pt[0][:, g % 2, 0:w], ps_t[:, g % 2, 0:w], ACT.Copy, scale=P_S) \
                    .then_inc(pt_high, 1)

            def copy_raw(m, u, c, band):
                if c > band:
                    t, (lo, width) = 2 * m + u, CHUNKS[c]
                    act.wait_ge(slot_free, NC * t + c + 1)
                    if c == band + 1 and not is_tile(m, u, 0):
                        act.wait_ge(raw_stored, 16 * t)
                    nc.scalar.activation(raw[:, lo - CHUNK:lo - CHUNK + width],
                                         slots[:, (NC * u + c) % 2, 0:width], ACT.Copy).then_inc(raw_copied, 1)

            def sum_degree(m, u):
                t = 2 * m + u
                if not (isinstance(m, int) and m == 0):
                    act.wait_ge(adj_loaded[u], 16 * m)
                if not is_tile(m, u, 0):
                    act.wait_ge(degree_ready, t)
                nc.scalar.activation(junk[:, :], adj[:, u, :], ACT.Copy, accum_out=degree[:, bass.ds(t, 1)]) \
                    .then_inc(degree_ready, 1)

            def first(m, u):
                for c in range(1, NC):
                    copy_raw(m, u, c, 0)
                for c in range(NC):
                    exp(m, u, c)
                act.wait_ge(z_all_max_ready, 1)
                nc.scalar.mul(z_neg_max[:, :], z_all_max[:, :], -1.0).then_inc(z_neg_max_ready, 1)
                act.wait_ge(z_neg_max_ready, 1)
                nc.scalar.activation(z_exp[:, :], z[:, :], ACT.Exp, bias=z_neg_max[:, :],
                                     accum_out=z_sum[:, :]).then_inc(z_exp_ready, 1)

            def both(m, u, band):
                back = before(m, u)
                sum_degree(*back)
                copy_raw(m, u, 1, band)
                high(*back, 0)
                copy_raw(m, u, 2, band)
                for c in range(NC):
                    high(*back, 2 * c + 1)
                    exp(m, u, c)
                    if 2 * c + 2 < NG:
                        high(*back, 2 * c + 2)

            def last(m, u):
                sum_degree(m, u)
                for g in range(NG):
                    high(m, u, g)

            tiles(act, first, both, last)

        @block.vector
        def _(dve):
            def mask(m, u, c):
                t, (lo, width) = 2 * m + u, CHUNKS[c]
                if c == 0:
                    dve.wait_ge(bias_ready, t + 1)
                wait_apart(dve, slot_full, NC * t + c + 1, norm.power_ready)
                nc.vector.tensor_tensor_reduce(
                    out=sc[:, u, lo:lo + width], in0=slots[:, (NC * u + c) % 2, 0:width],
                    in1=bias[:, lo:lo + width], scale=1.0 / (Q_S * Q_S), scalar=-3.0e38,
                    op0=ALU.add, op1=ALU.max, accum_out=mx[:, c:c + 1]).then_inc(slot_free, 1)
                if c == NC - 1:
                    dve.wait_ge(slot_free, NC * (t + 1))
                    if not is_tile(m, u, 0):
                        dve.wait_ge(exp_done, NC * t)
                    nc.vector.tensor_reduce(out=nmax[:, :], in_=mx[:, :], axis=AX.X, op=ALU.max, negate=True) \
                        .then_inc(nmax_ready, 1)

            def weigh(m, u, c):
                t, (lo, width) = 2 * m + u, CHUNKS[c]
                dve.wait_ge(exp_done, NC * t + c + 1)
                nc.vector.tensor_tensor(out=sc[:, u, lo:lo + width], in0=sc[:, u, lo:lo + width],
                                        in1=adj[:, u, lo:lo + width], op=ALU.mult).then_inc(weighed, 1)

            def scale(m, u):
                t = 2 * m + u
                nc.vector.tensor_reduce(out=ssum[:, :], in_=esum[:, u, :], axis=AX.X, op=ALU.add) \
                    .then_inc(ssum_ready, 1)
                dve.wait_ge(ssum_ready, t + 1)
                nc.vector.reciprocal(rinv[:, :], ssum[:, :]).then_inc(rinv_ready, 1)
                dve.wait_ge(rinv_ready, t + 1)
                nc.vector.scalar_tensor_tensor(out=rscale[:, u:u + 1], in0=rinv[:, :], scalar=1.0 / (P_S * V_S),
                                               in1=natt[:, bass.ds(t, 1)], op0=ALU.mult, op1=ALU.mult) \
                    .then_inc(rscale_ready, 1)

            def low(m, u, g):
                dve.wait_ge(pt_high, NG * (2 * m + u) + g + 1)
                w = P * len(GROUPS[g])
                nc.vector.scalar_tensor_tensor(
                    out=pt[1][:, g % 2, 0:w], in0=ps_t[:, g % 2, 0:w], scalar=P_S,
                    in1=pt[0][:, g % 2, 0:w], op0=ALU.mult, op1=ALU.subtract).then_inc(pt_low, 1)

            def finish(m, u):
                t = 2 * m + u
                dve.wait_ge(used, NG * (t + 1))
                dve.wait_ge(rscale_ready, t + 1)
                dve.wait_ge(xb_ready, t + 1)
                norm.free(dve, m, u)
                nc.vector.scalar_tensor_tensor(out=norm.r[:, :], in0=ps_o[:, u, :], scalar=rscale[:, u:u + 1],
                                               in1=xb[:, u, :], op0=ALU.mult, op1=ALU.add).then_inc(r_ready, 1)
                dve.wait_ge(r_ready, t + 1)
                norm.statistics(nc, dve, t)

            def first(m, u):
                for c in range(NC):
                    mask(m, u, c)
                for c in range(NC):
                    weigh(m, u, c)

            def node_attention():
                dve.wait_ge(z_all_sum_ready, 1)
                nc.vector.reciprocal(z_rinv[:, :], z_all_sum[:, :]).then_inc(z_rinv_ready, 1)
                dve.wait_ge(z_rinv_ready, 1)
                nc.vector.tensor_scalar(out=natt[:, :], in0=z_exp[:, :], scalar1=z_rinv[:, :], scalar2=None,
                                        op0=ALU.mult).then_inc(natt_ready, 1)
                dve.wait_ge(natt_ready, 1)

            def both(m, u, _band):
                back = before(m, u)
                for c in range(NC - 1):
                    mask(m, u, c)
                low(*back, 0)
                mask(m, u, NC - 1)
                for c in range(NC):
                    low(*back, 2 * c + 1)
                    if 2 * c + 2 < NG:
                        low(*back, 2 * c + 2)
                    weigh(m, u, c)
                if is_tile(m, u, 1):
                    node_attention()
                    scale(*back)
                scale(m, u)
                finish(*back)

            def last(m, u):
                for g in range(NG):
                    low(m, u, g)
                finish(m, u)

            nc.vector.tensor_reduce(out=z_max[:, :], in_=z[:, :], axis=AX.X, op=ALU.max) \
                .then_inc(z_max_ready, 1)
            tiles(dve, first, both, last)


def columns_of(adj_cols, t):
    return adj_cols[bass.ds(t, 1), :, :, :].rearrange("o p k q -> (o p) k q")


def aggregate(nc, layer, tag, x_rows, out_rows, adj_cols, a32, y, bias_row, ident, dcol=None):
    with ExitStack() as ctx:
        s = Scope(nc, ctx, tag, layer)
        a16 = s.sb("adj16", [P, 2, T, P], F16)
        xres = s.sb("xres", [P, 2, D])
        act_in = s.sb("act_in", [P, D])
        norm = Norm(s)
        ps = s.ps("ps", [P, 2, BANK])
        adj_loaded = [s.sem(f"adj_loaded{u}") for u in range(2)]
        xres_loaded = [s.sem(f"xres_loaded{u}") for u in range(2)]
        narrowed = s.sem("narrowed")
        diag_ready = s.sem("diag_ready")
        summed = s.sem("summed")
        biased = s.sem("biased")
        r_ready = s.sem("r_ready")
        block = ctx.enter_context(nc.Block())

        @block.sync
        def _(sp):
            def load(m, u):
                t = 2 * m + u
                if not (isinstance(m, int) and m == 0):
                    sp.wait_ge(narrowed, t - 1)
                    sp.dma_start(a32[:, u, :, :], columns_of(adj_cols, t)).then_inc(adj_loaded[u], 16)
                    sp.wait_ge(r_ready, t - 1)
                sp.dma_start(xres[:, u, :], x_rows[bass.ds(t * P, P), :]).then_inc(xres_loaded[u], 16)

            def late(m, u):
                load(m, u)
                norm.store(sp, out_rows, *before(*before(m, u)))

            load(0, 0)
            load(0, 1)
            pairs(sp, 2, T, late)
            norm.store(sp, out_rows, T // 2 - 1, 0)
            norm.store(sp, out_rows, T // 2 - 1, 1)
            norm.all_stored(sp)

        @block.gpsimd
        def _(pool):
            norm.exponent(nc, pool)
            norm.finish(nc, pool, 0, 0)
            norm.finish(nc, pool, 0, 1)
            pairs(pool, 2, T, lambda m, u: norm.finish(nc, pool, m, u))

        @block.scalar
        def _(act):
            def step(m, u):
                if not (isinstance(m, int) and m == 0):
                    act.wait_ge(adj_loaded[u], 16 * m)
                    act.wait_ge(summed, 2 * m + u - 1)
                nc.scalar.activation(a16[:, u, :, :], a32[:, u, :, :], ACT.Copy).then_inc(narrowed, 1)

            step(0, 0)
            step(0, 1)
            pairs(act, 2, T, step)

        @block.tensor
        def _(pe):
            def step(m, u):
                t = 2 * m + u
                pe.wait_ge(narrowed if dcol is None else diag_ready, t + 1)
                if not (isinstance(m, int) and m == 0):
                    pe.wait_ge(biased, t - 1)
                for k in range(T):
                    r = rows_of(k)
                    for b in range(2):
                        mm = nc.tensor.matmul(ps[:, u, :], a16[0:r, u, k, :], y[b][0:r, k, :],
                                              start=k == 0 and b == 0, stop=k == T - 1 and b == 1)
                mm.then_inc(summed, 1)

            step(0, 0)
            step(0, 1)
            pairs(pe, 2, T, step)

        @block.vector
        def _(dve):
            def identity(m, u):
                t = 2 * m + u
                dve.wait_ge(narrowed, t + 1)
                part = a16[:, u, bass.ds(t, 1), :].rearrange("p o q -> p (o q)")
                nc.vector.tensor_tensor(out=part, in0=part, in1=ident[:, :], op=ALU.add).then_inc(diag_ready, 1)

            def step(m, u):
                t = 2 * m + u
                dve.wait_ge(summed, t + 1)
                scale = 1.0 / V_S if dcol is None else dcol[:, bass.ds(t, 1)]
                nc.vector.scalar_tensor_tensor(out=act_in[:, :], in0=ps[:, u, :], scalar=scale,
                                               in1=bias_row[:, :], op0=ALU.mult, op1=ALU.add).then_inc(biased, 1)
                dve.wait_ge(biased, t + 1)
                dve.wait_ge(xres_loaded[u], 16 * m + 16)
                norm.free(dve, m, u)
                nc.vector.scalar_tensor_tensor(out=norm.r[:, :], in0=act_in[:, :], scalar=0.0,
                                               in1=xres[:, u, :], op0=ALU.max, op1=ALU.add).then_inc(r_ready, 1)
                dve.wait_ge(r_ready, t + 1)
                norm.statistics(nc, dve, t)

            if dcol is None:
                step(0, 0)
                pairs(dve, 1, T, step)
            else:
                def both(m, u):
                    identity(*after(m, u))
                    step(m, u)

                identity(0, 0)
                both(0, 0)
                pairs(dve, 1, T - 1, both)
                step(T // 2 - 1, 1)


def build(nc, x, adj, adj_cols, wk, wq, wv, wo, w1, b1, w2, b2, node_w, edge_w, w3, b3, out):
    xt_rows = nc.dram_tensor("xt_rows", [NP, 2 * D], F16).ap()
    scores_rows = nc.dram_tensor("scores_rows", [2 * CHUNK, N], F32).ap()
    x1, x2, x3 = (nc.dram_tensor(f"x{n}", [NP, D], F32).ap() for n in (1, 2, 3))
    with ExitStack() as outer:
        g = Scope(nc, outer, "all")
        ident = g.sb("ident", [P, P])
        b1_row, b2_row, b3_row, node_row = (g.sb(n, [P, D]) for n in ("b1_row", "b2_row", "b3_row", "node_row"))
        z, degree = g.sb("z", [P, T]), g.sb("degree", [P, T])
        dy, dout = g.sb("dy", [P, T]), g.sb("dout", [P, T])
        cleared, made = g.sem("cleared"), g.sem("made")
        with nc.Block() as block:
            @block.gpsimd
            def _(pool):
                nc.gpsimd.memset(ident[:, :], 0.0).then_inc(cleared, 1)
                nc.gpsimd.memset(z[:, :], -3.0e38).then_inc(made, 1)
                pool.wait_ge(cleared, 1)
                nc.gpsimd.affine_select(out=ident[:, :], in_=ident[:, :], compare_op=ALU.not_equal, fill=1.0,
                                        base=0, pattern=[[-1, P]], channel_multiplier=1).then_inc(made, 1)

        def parts(s, name):
            return [s.sb(f"{name}_{a}", [P, J, D], F16) for a in ("high", "low")]

        def split_rows(y):
            return lambda t, bank: [(bank, y[0][:, bass.ds(t, 1), :].rearrange("p o n -> p (o n)"),
                                     y[1][:, bass.ds(t, 1), :].rearrange("p o n -> p (o n)"), V_S * XW)]

        with ExitStack() as ctx:
            s = Scope(nc, ctx, "l0")
            kk = s.sb("kk", [P, H, NP], F16)
            vv = s.sb("vv", [P, T, H, P + 2], F16)
            query, output = parts(s, "wq"), parts(s, "wo")
            with ExitStack() as inner:
                w = Scope(nc, inner, "l0w")
                key, value = parts(w, "wk"), parts(w, "wv")

                def keys(t, bank):
                    part = bank.rearrange("p (c r) -> p c r", c=J)
                    return [(part[KD * e:KD * e + KD, :, :], kk[0:KD, e::2, bass.ds(t * P, P)],
                             kk[KD:P, e::2, bass.ds(t * P, P)], Q_S * XW) for e in range(2)]

                def values(t, bank):
                    part = bank.rearrange("p (h k) -> p h k", h=H)
                    dst = vv[:, bass.ds(t, 1), :, :].rearrange("p o h k -> p (o h) k")
                    return [(part, dst[:, :, KD:P], dst[:, :, 0:KD], V_S * XW)]

                project(nc, s, "p0", x, ident, [(wk, *key), (wv, *value)],
                        [("cols", *key, keys), ("rows", *value, values)], xt_rows=xt_rows,
                        later=[(wq, *query), (wo, *output)],
                        prefetch=[(row[:, :], vector.broadcast_to([P, D])) for row, vector in
                                  ((b1_row, b1), (b2_row, b2), (b3_row, b3), (node_row, node_w))])
            attention(nc, s, x, x1, xt_rows, adj, kk, vv, query, output, ident)

        with ExitStack() as ctx:
            s = Scope(nc, ctx, "l1")
            y, w = [s.sb(f"y{a}", [P, T, D], F16) for a in range(2)], parts(s, "w")
            a32 = s.sb("adj32", [P, 2, T, P])
            project(nc, s, "p1", x1, ident, [(w1, *w)], [("rows", *w, split_rows(y))],
                    prefetch=[(a32[:, t, :, :], columns_of(adj_cols, t)) for t in range(2)])
            aggregate(nc, s, "a1", x1, x2, adj_cols, a32, y, b1_row, ident)

        with ExitStack() as ctx:
            s = Scope(nc, ctx, "l2")
            ht = [s.sb(f"ht{a}", [P, J, NP], F16) for a in range(2)]
            sup = [s.sb(f"sup{a}", [P, T, D], F16) for a in range(2)]
            adj_tiles = s.sb("adj_tiles", [P, 2, N])
            with ExitStack() as inner:
                w = Scope(nc, inner, "l2w")
                edge, support = parts(w, "edge"), parts(w, "support")

                def columns(t, bank):
                    return [(bank.rearrange("p (c r) -> p c r", c=J), ht[0][:, :, bass.ds(t * P, P)],
                             ht[1][:, :, bass.ds(t * P, P)], Q_S * XW)]

                project(nc, s, "p2", x2, ident, [(edge_w, *edge), (w2, *support)],
                        [("cols", *edge, columns), ("rows", *support, split_rows(sup))], score=(node_row, z),
                        prefetch=[(adj_tiles[:, t, :], adj[t * P:(t + 1) * P, :]) for t in range(2)])
            edge_attention(nc, s, x2, x3, scores_rows, adj, adj_tiles, ht, sup, z, b2_row, degree, ident)

        with ExitStack() as ctx:
            s = Scope(nc, ctx, "l3")
            y, w = [s.sb(f"y{a}", [P, T, D], F16) for a in range(2)], parts(s, "w")
            a32 = s.sb("adj32", [P, 2, T, P])
            project(nc, s, "p3", x3, ident, [(w3, *w)], [("rows", *w, split_rows(y))], degrees=(degree, dy, dout),
                    prefetch=[(a32[:, t, :, :], columns_of(adj_cols, t)) for t in range(2)])
            aggregate(nc, s, "a3", x3, out, adj_cols, a32, y, b3_row, ident, dcol=dout)


def kernel(x, adj, L0_gnn_Wks, L0_gnn_Wqs, L0_gnn_Wvs, L0_gnn_Wo, L1_gnn_W, L1_gnn_b, L2_gnn_weight,
           L2_gnn_bias, L2_gnn_node_w, L2_gnn_edge_w, L3_gnn_W, L3_gnn_b):
    import concourse.bacc as bacc
    from concourse.bass_utils import run_bass_kernel_spmd

    def heads(w):
        return np.asarray(w).transpose(1, 0, 2).reshape(D, D)

    def padded(a, shape):
        out = np.zeros(shape, np.float32)
        out[:a.shape[0], :a.shape[1]] = a
        return out

    x, adj = np.asarray(x), np.asarray(adj)
    cols = padded(adj.T, (NP, NP)).reshape(T, P, T, P).transpose(2, 1, 0, 3)
    arrays = {
        "x": padded(x, (NP, D)), "adj": padded(adj, (NP, N)), "adj_cols": cols,
        "wk": heads(L0_gnn_Wks), "wq": heads(L0_gnn_Wqs), "wv": heads(L0_gnn_Wvs),
        "wo": np.asarray(L0_gnn_Wo).reshape(H * KD, D),
        "w1": np.asarray(L1_gnn_W).T, "b1": np.asarray(L1_gnn_b).reshape(1, D),
        "w2": np.asarray(L2_gnn_weight), "b2": np.asarray(L2_gnn_bias).reshape(1, D),
        "node_w": np.asarray(L2_gnn_node_w).reshape(1, D), "edge_w": np.asarray(L2_gnn_edge_w),
        "w3": np.asarray(L3_gnn_W).T, "b3": np.asarray(L3_gnn_b).reshape(1, D),
    }
    arrays = {k: np.ascontiguousarray(v) for k, v in arrays.items()}
    nc = bacc.Bacc("TRN2", target_bir_lowering=False, num_devices=1)
    args = {k: nc.dram_tensor(f"in_{k}", v.shape, F32, kind="ExternalInput").ap() for k, v in arrays.items()}
    out = nc.dram_tensor("out_rows", (NP, D), F32, kind="ExternalOutput").ap()
    build(nc, **args, out=out)
    result = run_bass_kernel_spmd(nc, [{f"in_{k}": v for k, v in arrays.items()}], core_ids=[0])
    return result.results[0]["out_rows"][:N]
```
